# Optimizing a Trainium2 kernel written in Bass

```python
import numpy as np
import jax
import jax.numpy as jnp

def _softmax(x, axis=-1):
    return jax.nn.softmax(x, axis=axis)

def _gelu(x):
    return jax.nn.gelu(x, approximate=True)

def _silu(x):
    return jax.nn.silu(x)

def _sigmoid(x):
    return jax.nn.sigmoid(x)

def _layernorm(x, axis=-1, eps=1e-05):
    m = jnp.mean(x, axis=axis, keepdims=True)
    v = jnp.var(x, axis=axis, keepdims=True)
    return (x - m) / jnp.sqrt(v + eps)

def _scatter_add(tgt, idx, src, axis=0):
    return tgt.at[idx].add(src)

def _segment_sum(src, seg, n):
    return jax.ops.segment_sum(src, seg, n)
kernel_name = 'mk_adj_ffn_d2_adj_r2_734776'

def setup_inputs(seed: int=0):
    np.random.seed(seed)
    _w = jnp.asarray

    def _rec_inputs():
        import jax
        import jax.numpy as jnp
        _gk = jax.random.key(seed)
        x = -0.000929 + 1 * jax.random.normal(jax.random.fold_in(_gk, 1), (2048, 128), jnp.float32)
        _a = jax.random.bernoulli(jax.random.fold_in(_gk, 2), 0.00195312, (2048, 2048))
        _a = jnp.logical_or(_a, jnp.eye(2048, dtype=bool))
        _af = _a.astype(jnp.float32)
        adj = _af
        return (x, adj)
    x, adj = _rec_inputs()

    def _L0_gnn_setup():
        import jax, jax.numpy as jnp
        import numpy as np
        ALPHA = 0.2
        NEG_INF = -9000000000000000.0
        LN_EPS = 1e-05
        N = 2048
        IN_F = 128
        OUT_F = 128
        HEADS = 4
        HEAD_DIM = OUT_F // HEADS
        EDGE_PROB = 0.02
        key = jax.random.key(seed)
        kx, ka, kw, kav = jax.random.split(key, 4)
        x = jax.random.normal(kx, (N, IN_F), dtype=jnp.float32)
        adj = jax.random.bernoulli(ka, EDGE_PROB, (N, N)).astype(jnp.float32)
        adj = jnp.maximum(adj, jnp.eye(N, dtype=jnp.float32))

        def xavier(k, shape, gain=1.414):
            fan_in, fan_out = (shape[0], shape[1])
            bound = gain * np.sqrt(6.0 / (fan_in + fan_out))
            return jax.random.uniform(k, shape, jnp.float32, -bound, bound)
        W = xavier(kw, (IN_F, OUT_F))
        a = xavier(kav, (2 * HEAD_DIM, 1))
        gamma = jnp.ones((OUT_F,), dtype=jnp.float32)
        beta = jnp.zeros((OUT_F,), dtype=jnp.float32)
        return {'x': x, 'adj': adj, 'W': W, 'a': a, 'gamma': gamma, 'beta': beta}
    _L0_gnn_all = _L0_gnn_setup()
    _L0_gnn_in = {k: v for k, v in _L0_gnn_all.items() if k in ('W', 'a', 'gamma', 'beta')}
    del _L0_gnn_all

    def _L0_ffn_setup():
        import jax, jax.numpy as jnp
        import numpy as np
        DIM = 128
        HEADS = 8
        NUM_KEYS = 128
        NUM_KV = NUM_KEYS ** 2
        PK_TOPK = 16
        FINAL_TOPK = 16
        DIM_KEY = DIM // 2
        P = 2

        def _pk(x, Wq_pk, pk_keys):
            b, n, _ = x.shape
            q = (x @ Wq_pk).reshape(b, n, P, HEADS, DIM_KEY).transpose(2, 0, 1, 3, 4)
            sim = jnp.einsum('pbnhd,pkhd->pbnhk', q, pk_keys)
            scores, idx = jax.lax.top_k(sim, PK_TOPK)
            idx0 = idx[0]
            idx1 = idx[1] * NUM_KEYS
            index = (idx0[..., :, None] + idx1[..., None, :]).reshape(b, n, HEADS, PK_TOPK * PK_TOPK)
            score = (scores[0][..., :, None] + scores[1][..., None, :]).reshape(b, n, HEADS, PK_TOPK * PK_TOPK)
            final_scores, pk_idx = jax.lax.top_k(score, FINAL_TOPK)
            final_indices = jnp.take_along_axis(index, pk_idx, axis=-1)
            final_scores = jax.nn.softmax(final_scores, axis=-1)
            return (final_scores, final_indices)
        key = jax.random.key(seed)
        ks = jax.random.split(key, 7)
        b, n = (2, 512)
        std = 0.02
        x = jax.random.normal(ks[0], (b, n, DIM), dtype=jnp.float32)
        Wq_pk = jax.random.normal(ks[1], (DIM, P * HEADS * DIM_KEY), dtype=jnp.float32) * std
        pk_keys = jax.random.normal(ks[2], (P, NUM_KEYS, HEADS, DIM_KEY), dtype=jnp.float32) * std
        Wq = jax.random.normal(ks[3], (DIM, HEADS * DIM), dtype=jnp.float32) * std
        keys_table = jax.random.normal(ks[4], (NUM_KV * HEADS, DIM), dtype=jnp.float32) * std
        values_table = jax.random.normal(ks[5], (NUM_KV * HEADS, DIM), dtype=jnp.float32) * std
        Wo = jax.random.normal(ks[6], (DIM * HEADS, DIM), dtype=jnp.float32) * std
        return {'x': x, 'Wq_pk': Wq_pk, 'pk_keys': pk_keys, 'Wq': Wq, 'keys_table': keys_table, 'values_table': values_table, 'Wo': Wo}
    _L0_ffn_all = _L0_ffn_setup()
    _L0_ffn_in = {k: v for k, v in _L0_ffn_all.items() if k in ('Wq_pk', 'pk_keys', 'Wq', 'keys_table', 'values_table', 'Wo')}
    del _L0_ffn_all

    def _L1_gnn_setup():
        import jax, jax.numpy as jnp
        import numpy as np
        N = 4096
        D = 128
        DENSITY = 0.02
        key = jax.random.key(seed)
        k1, k2, k3, k4 = jax.random.split(key, 4)
        inputs = jax.random.normal(k1, (N, D), dtype=jnp.float32)
        vals = jax.random.uniform(k2, (N, N), dtype=jnp.float32, minval=0.1, maxval=1.0)
        mask = jax.random.uniform(k3, (N, N), dtype=jnp.float32) < DENSITY
        adj = jnp.where(mask, vals, 0.0)
        H_v = 0.1 * jax.random.normal(k4, (D, 1), dtype=jnp.float32)
        return {'inputs': inputs, 'adj': adj, 'H_v': H_v}
    _L1_gnn_all = _L1_gnn_setup()
    _L1_gnn_in = {k: v for k, v in _L1_gnn_all.items() if k in ('H_v',)}
    del _L1_gnn_all

    def _L1_ffn_setup():
        import jax, jax.numpy as jnp
        import numpy as np
        B, K, D = (256, 16, 128)
        E = 32
        H = int(D * 0.25)
        key = jax.random.key(seed)
        ks = jax.random.split(key, 7)
        d_rs = D ** (-0.5)
        h_rs = H ** (-0.5)
        x = jax.random.normal(ks[0], (B, K, D), dtype=jnp.float32)
        router_w = jax.random.uniform(ks[1], (E, D), jnp.float32, -d_rs, d_rs)
        router_b = jax.random.uniform(ks[2], (E,), jnp.float32, -d_rs, d_rs)
        W1 = jax.random.uniform(ks[3], (E, D, H), jnp.float32, -h_rs, h_rs)
        b1 = jax.random.uniform(ks[4], (E, H), jnp.float32, -h_rs, h_rs)
        W2 = jax.random.uniform(ks[5], (E, H, D), jnp.float32, -d_rs, d_rs)
        b2 = jax.random.uniform(ks[6], (E, D), jnp.float32, -d_rs, d_rs)
        return {'x': x, 'router_w': router_w, 'router_b': router_b, 'W1': W1, 'b1': b1, 'W2': W2, 'b2': b2}
    _L1_ffn_all = _L1_ffn_setup()
    _L1_ffn_in = {k: v for k, v in _L1_ffn_all.items() if k in ('router_w', 'router_b', 'W1', 'b1', 'W2', 'b2')}
    del _L1_ffn_all
    return {'x': x, 'adj': adj, 'L0_gnn_W': _L0_gnn_in['W'], 'L0_gnn_a': _L0_gnn_in['a'], 'L0_gnn_gamma': _L0_gnn_in['gamma'], 'L0_gnn_beta': _L0_gnn_in['beta'], 'L0_ffn_Wq_pk': _L0_ffn_in['Wq_pk'], 'L0_ffn_pk_keys': _L0_ffn_in['pk_keys'], 'L0_ffn_Wq': _L0_ffn_in['Wq'], 'L0_ffn_keys_table': _L0_ffn_in['keys_table'], 'L0_ffn_values_table': _L0_ffn_in['values_table'], 'L0_ffn_Wo': _L0_ffn_in['Wo'], 'L1_gnn_H_v': _L1_gnn_in['H_v'], 'L1_ffn_router_w': _L1_ffn_in['router_w'], 'L1_ffn_router_b': _L1_ffn_in['router_b'], 'L1_ffn_W1': _L1_ffn_in['W1'], 'L1_ffn_b1': _L1_ffn_in['b1'], 'L1_ffn_W2': _L1_ffn_in['W2'], 'L1_ffn_b2': _L1_ffn_in['b2']}

def reference(x, adj, L0_gnn_W, L0_gnn_a, L0_gnn_gamma, L0_gnn_beta, L0_ffn_Wq_pk, L0_ffn_pk_keys, L0_ffn_Wq, L0_ffn_keys_table, L0_ffn_values_table, L0_ffn_Wo, L1_gnn_H_v, L1_ffn_router_w, L1_ffn_router_b, L1_ffn_W1, L1_ffn_b1, L1_ffn_W2, L1_ffn_b2):
    import jax
    import jax.numpy as jnp

    def _L0_gnn_ref(x, adj, W, a, gamma, beta):
        import jax, jax.numpy as jnp
        import numpy as np
        ALPHA = 0.2
        NEG_INF = -9000000000000000.0
        LN_EPS = 1e-05
        N = 2048
        IN_F = 128
        OUT_F = 128
        HEADS = 4
        HEAD_DIM = OUT_F // HEADS
        EDGE_PROB = 0.02
        n = x.shape[0]
        head_dim = a.shape[0] // 2
        heads = W.shape[1] // head_dim
        h = (x @ W).reshape(n, heads, head_dim)
        src = jnp.einsum('nhd,d->nh', h, a[:head_dim, 0])
        dst = jnp.einsum('nhd,d->nh', h, a[head_dim:, 0])
        e = src[:, :, None] + dst.T[None, :, :]
        e = jnp.where(e > 0, e, ALPHA * e)
        mask = adj[:, None, :] > 0
        e = jnp.where(mask, e, NEG_INF)
        attn = jax.nn.softmax(e, axis=-1)
        out = jnp.einsum('nhm,mhd->nhd', attn, h)
        out = out.reshape(n, heads * head_dim)
        mu = jnp.mean(out, axis=-1, keepdims=True)
        var = jnp.var(out, axis=-1, keepdims=True)
        out = (out - mu) / jnp.sqrt(var + LN_EPS) * gamma + beta
        return out

    def _L0_ffn_ref(x, Wq_pk, pk_keys, Wq, keys_table, values_table, Wo):
        import jax, jax.numpy as jnp
        import numpy as np
        DIM = 128
        HEADS = 8
        NUM_KEYS = 128
        NUM_KV = NUM_KEYS ** 2
        PK_TOPK = 16
        FINAL_TOPK = 16
        DIM_KEY = DIM // 2
        P = 2

        def _pk(x, Wq_pk, pk_keys):
            b, n, _ = x.shape
            q = (x @ Wq_pk).reshape(b, n, P, HEADS, DIM_KEY).transpose(2, 0, 1, 3, 4)
            sim = jnp.einsum('pbnhd,pkhd->pbnhk', q, pk_keys)
            scores, idx = jax.lax.top_k(sim, PK_TOPK)
            idx0 = idx[0]
            idx1 = idx[1] * NUM_KEYS
            index = (idx0[..., :, None] + idx1[..., None, :]).reshape(b, n, HEADS, PK_TOPK * PK_TOPK)
            score = (scores[0][..., :, None] + scores[1][..., None, :]).reshape(b, n, HEADS, PK_TOPK * PK_TOPK)
            final_scores, pk_idx = jax.lax.top_k(score, FINAL_TOPK)
            final_indices = jnp.take_along_axis(index, pk_idx, axis=-1)
            final_scores = jax.nn.softmax(final_scores, axis=-1)
            return (final_scores, final_indices)
        b, n, d = x.shape
        q = (x @ Wq).reshape(b, n, HEADS, DIM) * DIM ** (-0.5)
        kv_scores, indices = _pk(x, Wq_pk, pk_keys)
        offsets = jnp.arange(HEADS, dtype=indices.dtype) * NUM_KV
        ind = indices + offsets[None, None, :, None]
        k = jnp.einsum('bnhk,bnhkd->bnhd', kv_scores, keys_table[ind])
        v = jnp.einsum('bnhk,bnhkd->bnhd', kv_scores, values_table[ind])
        sim = jnp.einsum('bihd,bjhd->bhij', q, k)
        neg = -jnp.finfo(sim.dtype).max
        causal = jnp.tril(jnp.ones((n, n), dtype=bool))
        sim = jnp.where(causal, sim, neg)
        attn = jax.nn.softmax(sim, axis=-1)
        out = jnp.einsum('bhij,bjhd->bhid', attn, v)
        out = out.transpose(0, 2, 1, 3).reshape(b, n, HEADS * DIM)
        return out @ Wo

    def _L1_gnn_ref(inputs, adj, H_v):
        import jax, jax.numpy as jnp
        import numpy as np
        N = 4096
        D = 128
        DENSITY = 0.02
        scores = jnp.squeeze(inputs @ H_v, -1)
        mask = adj != 0.0
        logits = adj * scores[None, :]
        neg = jnp.asarray(jnp.finfo(logits.dtype).min, logits.dtype)
        logits = jnp.where(mask, logits, neg)
        m = jnp.max(logits, axis=1, keepdims=True)
        e = jnp.where(mask, jnp.exp(logits - m), 0.0)
        s = jnp.sum(e, axis=1, keepdims=True)
        weights = e / jnp.where(s > 0, s, 1.0)
        return weights @ inputs

    def _L1_ffn_ref(x, router_w, router_b, W1, b1, W2, b2):
        import jax, jax.numpy as jnp
        import numpy as np
        B, K, D = (256, 16, 128)
        E = 32
        H = int(D * 0.25)
        xf = x.reshape(-1, D)
        logits = xf @ router_w.T + router_b
        idx = jnp.argmax(logits, axis=-1)
        w1t = jnp.take(W1, idx, axis=0)
        h = jnp.einsum('nd,ndh->nh', xf, w1t) + jnp.take(b1, idx, axis=0)
        h = jax.nn.relu(h)
        w2t = jnp.take(W2, idx, axis=0)
        out = jnp.einsum('nh,nhd->nd', h, w2t) + jnp.take(b2, idx, axis=0)
        out = jax.nn.relu(out)
        return out.reshape(x.shape)
    x = x + _L0_gnn_ref(_layernorm(x, axis=-1), adj, L0_gnn_W, L0_gnn_a, L0_gnn_gamma, L0_gnn_beta)
    x = x + _L0_ffn_ref(_layernorm(x, axis=-1)[None], L0_ffn_Wq_pk, L0_ffn_pk_keys, L0_ffn_Wq, L0_ffn_keys_table, L0_ffn_values_table, L0_ffn_Wo)[0]
    x = x + _L1_gnn_ref(_layernorm(x, axis=-1), adj, L1_gnn_H_v)
    x = x + _L1_ffn_ref(_layernorm(x, axis=-1)[None], L1_ffn_router_w, L1_ffn_router_b, L1_ffn_W1, L1_ffn_b1, L1_ffn_W2, L1_ffn_b2)[0]
    return x

_drawn_inputs = setup_inputs


def setup_inputs(seed=0):
    import zlib

    import numpy as np

    out = dict(_drawn_inputs(seed))
    spreads = {'L0_gnn_gamma': (1.0, 0.2), 'L0_gnn_beta': (0.0, 0.1)}
    factors = {'L0_ffn_Wq_pk': 22.838,
     'L0_ffn_pk_keys': 8.0,
     'L0_ffn_Wq': 64.0,
     'L0_ffn_keys_table': 64.0,
     'L0_ffn_values_table': 8.0,
     'L0_ffn_Wo': 8.0,
     'L1_ffn_b1': 7.545,
     'L1_ffn_b2': 3.025}
    for name, (base, spread) in spreads.items():
        noise = np.random.default_rng([zlib.crc32(name.encode()), seed]).standard_normal(out[name].shape)
        drawn = base * np.exp(spread * noise) if base else spread * noise
        out[name] = jnp.asarray(drawn.astype(out[name].dtype))
    for name, factor in factors.items():
        out[name] = (out[name] * factor).astype(out[name].dtype)
    return out
```

```python
from contextlib import ExitStack

import concourse.bass as bass
from concourse import mybir
from concourse.alu_op_type import AluOpType as ALU

F32 = mybir.dt.float32
BF16 = mybir.dt.bfloat16
U32 = mybir.dt.uint32
I32 = mybir.dt.int32
ACT = mybir.ActivationFunctionType
AX = mybir.AxisListType.X
P = 128
EPS = 1e-5
HIDE = -1e30
ds = bass.ds


def plan_rounds(tiles):
    plan = [(r, 1) for r in range(-4, 0)]
    r = 0
    while r + 7 < tiles:
        plan.append((r, 4))
        r += 4
    return plan + [(q, 1) for q in range(r, tiles)]


def chunk_widths(first, rounds):
    blocks = first + rounds
    return [4] * (blocks // 4) + ([blocks % 4] if blocks % 4 else [])


def build_network(nc, x, adj, W, WT, a, gamma, beta, WqpkT, pkT, Wq, kv_table, Wo, Hv,
                  router_wT, router_b, W1, b1, W2, b2, out):
    N = x.shape[0]
    T = N // P
    GH, GD = 4, 32
    H, K = 8, 16
    E = router_wT.shape[1]
    EC = W1.shape[1] // P
    KEYS_PER_HEAD = kv_table.shape[0] // H
    ROW = kv_table.shape[1]
    STEPS = 4
    TOK = P // STEPS
    GROUP = 8
    GROUPS = TOK // GROUP
    SLOPE = 0.2
    plan = plan_rounds(T)

    def after(eng, sem, n):
        if not isinstance(n, int) or n > 0:
            eng.wait_ge(sem, n)

    def wait_alone(eng, sem, n):
        eng.wait_ge(sem, n)
        eng.sem_inc(passed, 1)

    chunks_before = [0]
    for first, rounds in plan:
        if first >= 0:
            for _ in range(rounds):
                chunks_before.append(chunks_before[-1] + H * len(chunk_widths(first, rounds)))

    x1_dram = nc.dram_tensor("x1_dram", [N, P], F32, kind="Internal").ap()
    x2_dram = nc.dram_tensor("x2_dram", [N, P], F32, kind="Internal").ap()

    with ExitStack() as ctx:
        def sb(name, shape, dt=F32):
            return ctx.enter_context(nc.sbuf_tensor(name, shape, dt))

        def sem(name):
            return ctx.enter_context(nc.semaphore(name))

        TILE_KV = 2 * H * P
        kv = sb("kv", [P, T, TILE_KV])
        last3 = kv[:, T - 3:T, :].rearrange("p t n -> p (t n)")
        h_all = last3[:, 0:N]
        masked_dst = last3[:, 2048:2048 + N]
        edge_hide = last3[:, 4096:5120].bitcast(BF16)[:, 0:N]
        dst3 = last3[0:96, 5120:6144].bitcast(BF16)[:, 0:N]
        xnT_all = kv[:, T - 4, 0:N]
        stage = sb("stage", [P, 2, H, P])
        ring = sb("ring", [P, 2, GROUP, ROW])
        mix_keys = sb("mix_keys", [P, 2048])
        xn1T = sb("xn1T", [P, T, P])
        att_p = sb("att_p", [P, max(N, 2048)])
        pt_sb = sb("pt_sb", [P, 2, 512])
        mask_wide = sb("mask_wide", [P, 896], BF16)
        wT = sb("wT", [P, 2, P])
        idxT = sb("idxT", [P, 2, P], U32)
        idx_now = sb("idx_now", [P, 2, 2 * GROUP], U32)
        w_block = sb("w_block", [P, 2, TOK, H])
        sims = sb("sims", [P, 4, P])
        scratch = sb("scratch", [P, 512])
        cand = sb("cand", [P, 2, K * K])
        ident = sb("ident", [P, P])
        identb = sb("identb", [P, P], BF16)
        sel_head = sb("sel_head", [96, GH, P], BF16)
        gamma_b = sb("gamma_b", [P, P])
        beta_b = sb("beta_b", [P, P])
        hv_b = sb("hv_b", [P, P])
        wq_pair = sb("wq_pair", [P, 2 * P])
        wo_pair = sb("wo_pair", [P, 2, P])
        qT = sb("qT", [P, 2, P])
        o_sb = sb("o_sb", [P, 2, P])
        y_acc = sb("y_acc", [P, P])
        xt = sb("xt", [P, P])
        x1 = sb("x1", [P, P])
        g_out = sb("g_out", [P, P])
        xn_tmp = sb("xn_tmp", [P, P])
        xT_pick = sb("xT_pick", [P, P])
        w_tile = sb("w_tile", [P, P])
        code_tile = sb("code_tile", [P, P])
        head_base = sb("head_base", [P, P])
        best = sb("best", [P, 2, 2, K])
        place = sb("place", [P, 2, 2, K], U32)
        placef = sb("placef", [P, 2, 2, K])
        top = sb("top", [P, 2, K])
        pos = sb("pos", [P, 2, K], U32)
        pos_hi = sb("pos_hi", [P, 2, K], U32)
        pos_lo = sb("pos_lo", [P, 2, K], U32)
        key0 = sb("key0", [P, 2, K])
        key1 = sb("key1", [P, 2, K])
        top_d = sb("top_d", [P, 2, K])
        top_e = sb("top_e", [P, 2, K])
        top_s = sb("top_s", [P, 2, 2])
        iota16 = sb("iota16", [P, K])
        iota32 = sb("iota32", [P, E])
        row_head = sb("row_head", [P, H])
        col_head = sb("col_head", [P, GH])
        a_col = sb("a_col", [P, 2])
        a_block = sb("a_block", [P, 2 * GH])
        wa = sb("wa", [P, 2 * GH])
        src_dst = sb("src_dst", [P, T, 2 * GH])
        src_now = sb("src_now", [P, 1])
        gs = sb("gs", [P, 6])
        gat_sum = sb("gat_sum", [P, 1])
        att_m = sb("att_m", [P, 2])
        att_nm = sb("att_nm", [P, 2])
        att_sum = sb("att_sum", [P, 2])
        att_r = sb("att_r", [P, 2])
        stats = sb("stats", [P, T, 6])
        moments = sb("moments", [P, T, 2])
        rs = sb("rs", [P, 4, T])
        rs_i = sb("rs_i", [P, 2, T], I32)
        scores = sb("scores", [P, T])
        mix_m = sb("mix_m", [P, 4])
        mix_nm = sb("mix_nm", [P, 4])
        mix_any = sb("mix_any", [P, 4])
        mix_sum = sb("mix_sum", [P, 4])
        mix_r = sb("mix_r", [P, 4])
        oT_sb = qT
        ln_tmp = scratch[:, 0:P]
        x_all = ring[:, :, :, :].rearrange("p s g n -> p (s g n)")[:, 0:N].rearrange("p (t d) -> p t d", d=P)
        wqpkT_sb = stage[0:64, :, :, :].rearrange("p k h n -> p (k h n)")
        pkT_sb = att_p[0:64, 0:2048]
        wt_sb = g_out
        gat_w = xn_tmp
        iota_i = cand[:, 0, 0:P].bitcast(I32)
        dst_parts = w_block[:, :, :, :].rearrange("p b t h -> p (b t h)")
        dst_nat = sims[:, :, :].rearrange("p a n -> p (a n)").bitcast(BF16)
        dst_nat2 = scratch[:, :].bitcast(BF16)
        free = kv[:, :, :].rearrange("p t n -> p (t n)")
        adj_sb = free[:, 0:4096].rearrange("p (b n) -> p b n", b=2)
        logit = free[:, 4096:8192].rearrange("p (b n) -> p b n", b=2)
        score_b = free[:, 8192:8192 + N]
        hid = free[:, 10240:10240 + EC * 512].rearrange("p (c n) -> p c n", c=EC)
        w1_sb = mix_keys[:, 0:E * 32]
        w2_sb = mix_keys[:, 1024:2048].rearrange("p (c n) -> p c n", c=EC)
        b1_sb = sb("b1_sb", [P, EC])
        b2_sb = xt[0:E, :]
        rw_sb = code_tile[:, 0:E]
        rb_sb = code_tile[:, E:2 * E]
        sel_expert = cand[0:E, :, :].rearrange("p a n -> p (a n)").bitcast(BF16).rearrange("p (c n) -> p c n", c=EC)
        x3 = stage[:, 0, 0:4, :]
        y_moe = stage[:, 0, 4:8, :]
        xn3T = stage[:, 1, 0:4, :]
        x2_in = stage[:, 1, 4:8, :]
        onehotT = scratch[0:E, :]
        onehotTb = sims[0:E, :, :].rearrange("p a n -> p (a n)").bitcast(BF16)[:, 0:512]
        xn3 = free[:, 10240:10752].rearrange("p (j n) -> p j n", j=4)
        onehot = w_tile[:, :].rearrange("p (j e) -> p j e", j=4)
        rlog = ln_tmp[:, :].rearrange("p (j e) -> p j e", j=4)
        rtop = best[:, :, :, :].rearrange("p a b k -> p (a b k)")[:, 0:32].rearrange("p (j k) -> p j k", j=4)
        rpos = place[:, :, :, :].rearrange("p a b k -> p (a b k)")[:, 0:32].rearrange("p (j k) -> p j k", j=4)
        rposf = placef[:, :, :, :].rearrange("p a b k -> p (a b k)")[:, 0:32].rearrange("p (j k) -> p j k", j=4)

        wide = ctx.enter_context(nc.psum_tensor("wide", [P, 2048], F32))
        turn = [ctx.enter_context(nc.psum_tensor(f"turn{i}", [P, 512], F32)) for i in range(2)]
        rowsum = ctx.enter_context(nc.psum_tensor("rowsum", [P, 512], F32))
        acc = ctx.enter_context(nc.psum_tensor("acc", [P, 512], F32))
        turnb = [t[:, :].bitcast(BF16) for t in turn]

        (c_mem, c_ln, c_x, c_w, c_pk, c_ab, c_ablock, c_adj, c_ident, c_wa_in, c_wa, c_wa_sb, c_mix, c_mix_sb, c_xn, c_xT,
         c_xT_sb, c_h, c_sd, c_h_sb, c_sd_sb, c_d3, c_d3_sb, c_hide, c_pool, c_zero) = [
            sem("start_" + n) for n in
            "mem ln x w pk ab ablock adj ident wa_in wa wa_sb mix mix_sb xn xT xT_sb h sd h_sb sd_sb d3 d3_sb hide pool zero".split()]
        dst_shown, dst_used, gat_logit, gat_exp, gat_turned, gat_copied, gat_summed, gat_out = [
            sem("gat_" + n) for n in "shown used logit exp turned copied summed out".split()]
        sims_made, sims_in, picks_done, top_ready, top_exp = [
            sem("pick_" + n) for n in "made in done top exp".split()]
        codes_ready, codes_turned, idx_ready, idx_copied, idx_staged = [
            sem("code_" + n) for n in "ready turned idx copied staged".split()]
        row_in = [sem(f"row_in{i}") for i in range(2)]
        rows_used, rows_out, wblock_ready = [sem("rows_" + n) for n in "used out wblock".split()]
        v_turned, v_kept, k_kept = [sem("kv_" + n) for n in "vturned vkept kkept".split()]
        wq_in, wo_in, q_made, q_in, s_made, s_max, p_made, p_turned, p_copied, o_made, o_in, oT_made, oT_in, y_made, \
            y_used = [sem("att_" + n) for n in
                      "wqin woin qmade qin smade smax p turned copied omade oin oTmade oTin ymade yused".split()]
        xt_in, adj_in, hide_ready, x1_made, x1_out, xn1_made, xn1T_made, xn1T_in = [
            sem("mid_" + n) for n in "xt adj hide x1 x1out xn1 xn1T xn1Tin".split()]
        t_w, t_sel, t_x2, t_adj0, t_adj1, t_out = [sem("last_" + n) for n in "w sel x2 adj0 adj1 out".split()]
        score_rows, score_shown, score_in, mix_logit, mix_exp, mix_turned, mix_copied, mix_summed, x3_made = [
            sem("mix_" + n) for n in "rows shown in logit exp turned copied summed x3".split()]
        xn3_made, xn3T_made, xn3T_in, route_made, route_hot, hot_turned, hot_in, hid_made, hid_relu, hid_masked, \
            moe_made, moe_relu, moe_out = [sem("moe_" + n) for n in
            "xn3 xn3T xn3Tin route hot turned in hid relu masked made relu2 out".split()]
        t_adj = [t_adj0, t_adj1]
        passed = sem("passed")
        x1_back, x2_made, x2_out, xn2_made = [sem("end_" + n) for n in "x1back x2 x2out xn2".split()]

        def stages(first, rounds, i):
            t = first + i
            has = lambda off: 0 <= first + off and first + rounds - 1 + off < T
            return {
                "graph": t + 4 if has(4) else None,
                "pick": t + 3 if has(3) else None,
                "fetch": t + 1 if has(1) else None,
                "attend": t if has(0) else None,
                "widths": chunk_widths(first, rounds) if has(0) else None,
                "chunks": (chunks_before[first] + (H * len(chunk_widths(first, rounds))) * i) if has(0) else None,
                "whole": rounds > 1,
                "i": i,
            }

        def every_round(eng, body):
            for first, rounds in plan:
                if rounds == 1:
                    body(stages(first, rounds, 0))
                else:
                    with eng.Fori(0, rounds) as i:
                        body(stages(first, rounds, i))

        def tail_sync(sp):
            sp.wait_ge(sims_made, STEPS * T)
            sp.dma_start(w1_sb, W1).then_inc(t_w, 16)
            sp.dma_start(w2_sb, W2.rearrange("(c p) n -> p c n", p=P)).then_inc(t_w, 16)
            sp.wait_ge(codes_turned, T)
            sp.dma_start(rw_sb, router_wT).then_inc(t_w, 16)
            sp.dma_start(rb_sb, router_b.partition_broadcast(P)).then_inc(t_w, 16)
            sp.wait_ge(x1_made, T)
            sp.dma_start(b2_sb, b2).then_inc(t_w, 16)
            sp.wait_ge(xn2_made, T)
            sp.wait_ge(x2_out, 16 * T)
            with sp.Fori(0, T // 4) as u:
                sp.wait_ge(x3_made, 2 + 4 * u)
                sp.dma_start(x2_in, x2_dram.rearrange("(t p) d -> p t d", p=P)[:, ds(4 * u, 4), :]).then_inc(t_x2, 16)
                for j in range(4):
                    i = 4 * u + j
                    sp.wait_ge(mix_logit, 2 + i - 1)
                    sp.dma_start(adj_sb[:, j % 2, 0:N], adj[ds(i * P, P), :]).then_inc(t_adj[j % 2], 16)

        def tail_pool(pool):
            pool.wait_ge(picks_done, STEPS * T)
            pool.memset(sel_expert, 0.0).then_inc(c_pool, 1)
            pool.wait_ge(c_pool, 4)
            pool.affine_select(out=sel_expert.rearrange("e c (q n) -> e c q n", q=4),
                               in_=sel_expert.rearrange("e c (q n) -> e c q n", q=4),
                               compare_op=ALU.not_equal, fill=1.0, base=0,
                               pattern=[[-4, EC], [-1, 4], [0, 32]], channel_multiplier=1).then_inc(t_sel, 1)
            with pool.Fori(0, T // 4) as u:
                pool.wait_ge(moe_out, u + 1)
                pool.dma_start(out.rearrange("(t p) d -> p t d", p=P)[:, ds(4 * u, 4), :], y_moe).then_inc(t_out, 16)
            pool.wait_ge(t_out, 16 * (T // 4))

        def tail_tensor(pe, turn_and_sum):
            pe.wait_ge(score_rows, 1)
            for t in range(T):
                mm = pe.matmul(wide[:, t * P:(t + 1) * P], att_p[:, t * P:(t + 1) * P], ident[:, :],
                               start=True, stop=True)
            mm.then_inc(score_shown, 1)
            pe.wait_ge(score_in, 1)
            pe.wait_ge(t_w, 16 * 5)
            pe.wait_ge(t_sel, 1)
            with pe.Fori(0, T // 4) as u:
                for j in range(4):
                    i = 4 * u + j
                    pe.wait_ge(mix_exp, i + 1)
                    pe.wait_ge(x3_made, 2 + i - 1)
                    turn_and_sum(logit[:, j % 2, :], [4] * (N // 512), mix_turned, mix_copied, i * (N // 512),
                                 lambda b: xn1T[:, b, :], (acc, rowsum)[j % 2][:, 0:P]).then_inc(mix_summed, 1)
                pe.wait_ge(xn3_made, u + 1)
                for j in range(4):
                    mm = pe.transpose(turn[0][:, j * P:(j + 1) * P], xn3[:, j, :], ident[:, :])
                mm.then_inc(xn3T_made, 1)
                pe.wait_ge(xn3T_in, u + 1)
                for j in range(4):
                    mm = pe.matmul(turn[1][:, j * E:(j + 1) * E], xn3T[:, j, :], rw_sb, start=True, stop=True)
                mm.then_inc(route_made, 1)
                pe.wait_ge(route_hot, u + 1)
                for j in range(4):
                    mm = pe.transpose(turn[0][0:E, j * P:(j + 1) * P], onehot[:, j, :], ident[:, :])
                mm.then_inc(hot_turned, 1)
                pe.wait_ge(hot_in, u + 1)
                for c in range(EC):
                    pe.wait_ge(hid_masked, 2 + EC * u + c - 1)
                    b = c % 2
                    pe.matmul(wide[:, b * 512:(b + 1) * 512], w1_sb[:, c * P:(c + 1) * P],
                              xn3T.rearrange("p j n -> p (j n)"), start=True, stop=True)
                    pe.matmul(wide[:, 1024 + b * 512:1536 + b * 512], sel_expert[:, c, :], onehotTb,
                              start=True, stop=True).then_inc(hid_made, 1)
                pe.wait_ge(hid_masked, 2 + EC * (u + 1))
                for j in range(4):
                    dst = turn[1][:, j * P:(j + 1) * P]
                    pe.matmul(dst, onehotT[:, j * P:(j + 1) * P], b2_sb, start=True, stop=False)
                    for c in range(EC):
                        mm = pe.matmul(dst, hid[:, c, j * P:(j + 1) * P], w2_sb[:, c, :], start=False, stop=(c == EC - 1))
                mm.then_inc(moe_made, 1)
                pe.wait_ge(moe_relu, u + 1)

        def tail_scalar(act, copy_chunks):
            act.wait_ge(score_shown, 1)
            act.activation(score_b, wide[:, 0:N], ACT.Copy).then_inc(score_in, 1)
            with act.Fori(0, T // 4) as u:
                for j in range(4):
                    i = 4 * u + j
                    act.wait_ge(mix_logit, 2 + i + 1)
                    act.activation(logit[:, j % 2, 0:N], logit[:, j % 2, 0:N], ACT.Exp, bias=mix_nm[:, j:j + 1],
                                   accum_out=mix_sum[:, j:j + 1]).then_inc(mix_exp, 1)
                    copy_chunks([4] * (N // 512), mix_turned, mix_copied, i * (N // 512))
                act.wait_ge(xn3T_made, u + 1)
                act.activation(xn3T, turn[0][:, :].rearrange("p (j n) -> p j n", j=4), ACT.Copy).then_inc(xn3T_in, 1)
                act.wait_ge(hot_turned, u + 1)
                act.activation(onehotT, turn[0][0:E, :], ACT.Copy)
                act.activation(onehotTb, turn[0][0:E, :], ACT.Copy).then_inc(hot_in, 1)
                for c in range(EC):
                    act.wait_ge(hid_made, EC * u + c + 1)
                    act.activation(hid[:, c, :], wide[:, (c % 2) * 512:(c % 2 + 1) * 512], ACT.Relu,
                                   bias=b1_sb[:, c:c + 1]).then_inc(hid_relu, 1)
                act.wait_ge(moe_made, u + 1)
                act.wait_ge(t_out, 16 * u)
                act.activation(y_moe, turn[1][:, :].rearrange("p (j n) -> p j n", j=4), ACT.Relu).then_inc(moe_relu, 1)

        def tail_vector(dve, inverse_root):
            dve.sem_inc(mix_logit, 2)
            dve.sem_inc(x3_made, 2)
            dve.sem_inc(hid_masked, 2)
            dve.drain()
            dve.tensor_copy(att_p[:, 0:N].rearrange("p (t n) -> p t n", n=P),
                            scores[:, :].rearrange("p (t o) -> p t o", o=1).to_broadcast([P, T, P]))\
               .then_inc(score_rows, 1)
            dve.wait_ge(score_in, 1)
            dve.wait_ge(t_w, 16 * 5)

            def mix_logits(u, j):
                b = j % 2
                dve.wait_ge(t_adj[b], 16 * (2 * u + j // 2 + 1))
                dve.tensor_tensor(logit[:, b, 0:N], adj_sb[:, b, 0:N], score_b, ALU.mult)
                dve.drain()
                dve.tensor_scalar(adj_sb[:, b, 0:N], adj_sb[:, b, 0:N], 0.0, HIDE, ALU.is_equal, ALU.mult)
                dve.drain()
                dve.tensor_tensor_reduce(logit[:, b, 0:N], logit[:, b, 0:N], adj_sb[:, b, 0:N], 1.0, -3e38, ALU.add,
                                         ALU.max, mix_m[:, j:j + 1])
                dve.drain()
                dve.tensor_scalar(mix_any[:, j:j + 1], mix_m[:, j:j + 1], HIDE / 2, None, ALU.is_gt)
                dve.tensor_scalar(mix_nm[:, j:j + 1], mix_m[:, j:j + 1], -1.0, None, ALU.mult).then_inc(mix_logit, 1)

            def mix_out(u, j):
                i = 4 * u + j
                dve.wait_ge(mix_exp, i + 1)
                dve.reciprocal(mix_r[:, j:j + 1], mix_sum[:, j:j + 1])
                dve.drain()
                dve.tensor_tensor(mix_r[:, j:j + 1], mix_r[:, j:j + 1], mix_any[:, j:j + 1], ALU.mult)
                dve.drain()
                dve.wait_ge(mix_summed, i + 1)
                dve.scalar_tensor_tensor(x3[:, j, :], (acc, rowsum)[j % 2][:, 0:P], mix_r[:, j:j + 1], x2_in[:, j, :],
                                         ALU.mult, ALU.add).then_inc(x3_made, 1)

            with dve.Fori(0, T // 4) as u:
                mix_logits(u, 0)
                mix_logits(u, 1)
                dve.wait_ge(t_x2, 16 * (u + 1))
                for j in range(4):
                    mix_out(u, j)
                    if j < 2:
                        mix_logits(u, j + 2)
                dve.drain()
                for j in range(4):
                    dve.bn_stats(stats[:, j, :], x3[:, j, :])
                dve.drain()
                for j in range(4):
                    dve.bn_aggr(moments[:, j, :], stats[:, j, :])
                dve.drain()
                y = inverse_root(moments[:, 0:4, 1], 4)
                for j in range(4):
                    last = dve.tensor_scalar(xn3[:, j, :], x3[:, j, :], moments[:, j, 0:1], y[:, j:j + 1],
                                             ALU.subtract, ALU.mult)
                last.then_inc(xn3_made, 1)
                dve.wait_ge(route_made, u + 1)
                dve.tensor_tensor(rlog, turn[1][:, 0:4 * E].rearrange("p (j e) -> p j e", j=4),
                                  rb_sb.rearrange("p (o e) -> p o e", o=1).to_broadcast([P, 4, E]), ALU.add)
                dve.drain()
                for j in range(4):
                    dve.max(rtop[:, j, :], rlog[:, j, :])
                dve.drain()
                for j in range(4):
                    dve.max_index(rpos[:, j, :], rtop[:, j, :], rlog[:, j, :])
                dve.drain()
                dve.tensor_copy(rposf, rpos)
                dve.drain()
                dve.tensor_tensor(onehot, iota32[:, :].rearrange("p (o e) -> p o e", o=1).to_broadcast([P, 4, E]),
                                  rposf[:, :, 0:1].to_broadcast([P, 4, E]), ALU.is_equal).then_inc(route_hot, 1)
                for c in range(EC):
                    dve.wait_ge(hid_relu, EC * u + c + 1)
                    dve.tensor_tensor(hid[:, c, :], hid[:, c, :], wide[:, 1024 + (c % 2) * 512:1536 + (c % 2) * 512],
                                      ALU.mult).then_inc(hid_masked, 1)
                dve.wait_ge(moe_relu, u + 1)
                dve.tensor_tensor(y_moe, y_moe, x3, ALU.add).then_inc(moe_out, 1)
                dve.drain()

        block = ctx.enter_context(nc.Block())

        @block.sync
        def _(sp):
            xr = x.rearrange("(t p) d -> p t d", p=P)
            sp.dma_start(x_all, xr).then_inc(c_x, 16)
            sp.dma_start(wt_sb[:, :], WT).then_inc(c_wa_in, 16)
            for q in range(4):
                sp.dma_start(a_col[32 * q:32 * q + 32, :], a).then_inc(c_ab, 16)
            sp.dma_start(gat_w[:, :], W).then_inc(c_w, 16)
            sp.dma_start(wqpkT_sb, WqpkT).then_inc(c_pk, 16)
            sp.dma_start(pkT_sb, pkT).then_inc(c_pk, 16)
            sp.dma_start(masked_dst, adj[0:P, :]).then_inc(c_adj, 16)
            sp.dma_start(gamma_b[:, :], gamma.partition_broadcast(P)).then_inc(c_mem, 16)
            sp.dma_start(beta_b[:, :], beta.partition_broadcast(P)).then_inc(c_mem, 16)
            sp.dma_start(hv_b[:, :], Hv.rearrange("d o -> (d o)").partition_broadcast(P)).then_inc(c_mem, 16)
            sp.dma_start(b1_sb[:, :], b1).then_inc(c_mem, 16)

            def one_round(st):
                g, t = st["graph"], st["attend"]
                if g is not None:
                    after(sp, x1_made, g)
                    sp.dma_start(xt[:, :], x[ds(g * P, P), :]).then_inc(xt_in, 16)
                if t is not None:
                    after(sp, x2_out, 16 * t)
                    after(sp, xn2_made, t)
                    sp.wait_ge(x1_out, 16 * (t + 1))
                    sp.dma_start(y_acc[:, :], x1_dram[ds(t * P, P), :]).then_inc(x1_back, 16)
                    with sp.Fori(0, STEPS) as s:
                        n = STEPS * t + s
                        after(sp, q_made, n)
                        sp.dma_start(wq_pair[:, :], Wq[:, ds(s * 2 * P, 2 * P)]).then_inc(wq_in, 16)
                        after(sp, y_made, n)
                        sp.dma_start(wo_pair[:, :, :], Wo.rearrange("(h p) d -> p h d", p=P)[:, ds(2 * s, 2), :])\
                          .then_inc(wo_in, 16)
                if g is not None:
                    sp.wait_ge(gat_summed, STEPS * (g + 1))
                    sp.dma_start(masked_dst, adj[ds((g + 1) % T * P, P), :]).then_inc(adj_in, 16)
                    sp.wait_ge(x1_made, g + 1)
                    sp.dma_start(x1_dram[ds(g * P, P), :], x1[:, :]).then_inc(x1_out, 16)
                if t is not None:
                    sp.wait_ge(x2_made, t + 1)
                    sp.dma_start(x2_dram[ds(t * P, P), :], y_acc[:, :]).then_inc(x2_out, 16)

            every_round(sp, one_round)
            tail_sync(sp)

        @block.gpsimd
        def _(pool):
            pool.memset(ident[:, :], 0.0)
            pool.memset(row_head[:, :], 1.0)
            pool.memset(col_head[:, :], 1.0)
            pool.memset(mask_wide[:, :], 0.0)
            pool.memset(sel_head[:, :, :], 0.0)
            pool.iota(iota_i[:, :], [[KEYS_PER_HEAD, H], [0, K]], base=0, channel_multiplier=0).then_inc(c_pool, 1)
            pool.wait_ge(c_pool, 1)
            pool.affine_select(out=ident[:, :], in_=ident[:, :], compare_op=ALU.not_equal, fill=1.0, base=0,
                               pattern=[[-1, P]], channel_multiplier=1)
            pool.affine_select(out=row_head[:, :], in_=row_head[:, :], compare_op=ALU.is_ge, fill=0.0, base=0,
                               pattern=[[-K, H]], channel_multiplier=1)
            pool.affine_select(out=col_head[:, :], in_=col_head[:, :], compare_op=ALU.is_ge, fill=0.0, base=0,
                               pattern=[[-GD, GH]], channel_multiplier=1)
            pool.affine_select(out=mask_wide[:, :], in_=mask_wide[:, :], compare_op=ALU.is_ge, fill=HIDE, base=384,
                               pattern=[[-1, 896]], channel_multiplier=1)
            pool.affine_select(out=sel_head[:, :, :], in_=sel_head[:, :, :], compare_op=ALU.not_equal, fill=1.0,
                               base=0, pattern=[[-1, GH], [0, P]], channel_multiplier=1)
            pool.tensor_copy(head_base[:, :], iota_i[:, :]).then_inc(c_pool, 1)
            pool.wait_ge(c_pool, 2)
            pool.affine_select(out=row_head[:, :], in_=row_head[:, :], compare_op=ALU.is_ge, fill=0.0, base=K - 1,
                               pattern=[[K, H]], channel_multiplier=-1)
            pool.affine_select(out=col_head[:, :], in_=col_head[:, :], compare_op=ALU.is_ge, fill=0.0, base=GD - 1,
                               pattern=[[GD, GH]], channel_multiplier=-1)
            pool.affine_select(out=sel_head[:, :, :], in_=sel_head[:, :, :], compare_op=ALU.not_equal, fill=1.0,
                               base=-32, pattern=[[-1, GH], [0, P]], channel_multiplier=1)
            pool.iota(iota_i[:, :], [[1, P]], base=0, channel_multiplier=0)
            pool.tensor_copy(identb[:, :], ident[:, :]).then_inc(c_pool, 1)
            pool.wait_ge(c_pool, 3)
            pool.affine_select(out=sel_head[:, :, :], in_=sel_head[:, :, :], compare_op=ALU.not_equal, fill=1.0,
                               base=-64, pattern=[[-1, GH], [0, P]], channel_multiplier=1)
            pool.tensor_copy(iota16[:, :], iota_i[:, 0:K])
            pool.tensor_copy(iota32[:, :], iota_i[:, 0:E]).then_inc(c_ident, 1)
            pool.memset(kv[:, 0:T - 4, :], 0.0).then_inc(c_zero, 1)

            def one_round(st):
                r = st["fetch"]
                if r is None:
                    return
                wait_alone(pool, idx_ready, r + 1)
                with pool.Fori(0, STEPS) as s:
                    n = STEPS * r + s
                    for half in range(2):
                        pool.wait_ge(rows_used, 2 + GROUPS * n - 2 + 2 * half)
                        pool.tensor_copy(idx_now[:, half, :],
                                         idxT[:, ds(r % 2, 1), ds(s * TOK + half * 2 * GROUP, 2 * GROUP)])\
                            .then_inc(idx_copied, 1)
                        pool.wait_ge(idx_copied, 2 * n + half + 1)
                        for slot in range(2):
                            wait_alone(pool, rows_used, 2 + GROUPS * n + 2 * half + slot - 1)
                            for k in range(GROUP):
                                pool.indirect_dma_start(
                                    ring[:, slot, k, :], None, kv_table,
                                    bass.IndirectOffsetOnAxis(idx_now[:, half, slot * GROUP + k:slot * GROUP + k + 1], 0),
                                ).then_inc(row_in[slot], 16)

            every_round(pool, one_round)
            tail_pool(pool)

        @block.tensor
        def _(pe):
            pe.sem_inc(rows_used, 2)
            pe.wait_ge(c_pk, 32)
            for c in range(2 * H):
                mm = pe.matmul(wide[:, c * P:(c + 1) * P], wqpkT_sb[:, c * P:(c + 1) * P],
                               pkT_sb[:, c * P:(c + 1) * P], start=True, stop=True)
            mm.then_inc(c_mix, 1)
            pe.wait_ge(c_wa_in, 16)
            pe.wait_ge(c_ablock, 1)
            pe.matmul(acc[:, 0:2 * GH], wt_sb[:, :], a_block[:, :], start=True, stop=True).then_inc(c_wa, 1)
            pe.wait_ge(c_xn, 1)
            pe.wait_ge(c_ident, 1)
            pe.wait_ge(c_mix_sb, 1)
            for t in range(T):
                mm = pe.transpose(wide[:, t * P:(t + 1) * P], x_all[:, t, :], ident[:, :])
            mm.then_inc(c_xT, 1)
            pe.wait_ge(c_xT_sb, 1)
            pe.wait_ge(c_wa_sb, 1)
            for t in range(T):
                mm = pe.matmul(acc[:, t * 8:t * 8 + 8], xnT_all[:, t * P:(t + 1) * P], wa[:, :], start=True, stop=True)
            mm.then_inc(c_sd, 1)
            pe.wait_ge(c_w, 16)
            for t in range(T):
                mm = pe.matmul(wide[:, t * P:(t + 1) * P], xnT_all[:, t * P:(t + 1) * P], gat_w[:, :],
                               start=True, stop=True)
            mm.then_inc(c_h, 1)
            pe.wait_ge(c_sd_sb, 1)
            for t in range(T):
                nat = (dst_nat if t < 8 else dst_nat2)[:, (t % 8) * 96:(t % 8) * 96 + 96]
                mm = pe.transpose(turnb[t // 8][0:96, (t % 8) * P:(t % 8 + 1) * P], nat, identb[:, :])
            mm.then_inc(c_d3, 1)
            pe.wait_ge(c_d3_sb, 1)
            pe.wait_ge(c_h_sb, 1)

            def fetch_group(r, s, j):
                n = STEPS * r + s
                pe.wait_ge(row_in[j % 2], 16 * GROUP * (2 * n + j // 2 + 1))
                pe.wait_ge(wblock_ready, n + 1)
                after(pe, rows_out, GROUPS * n + j)
                for k in range(GROUP):
                    for part in range(2):
                        mm = pe.matmul(rowsum[:, part * 64 + k * H:part * 64 + (k + 1) * H],
                                       ring[:, j % 2, k, part * P:(part + 1) * P],
                                       w_block[:, ds(s % 2, 1), j * GROUP + k, :],
                                       start=True, stop=True)
                mm.then_inc(rows_used, 1)

            def turn_and_sum(probs, widths, turned, copied, count, rhs, dst):
                def turns(q):
                    for b in range(widths[q]):
                        col = (4 * q + b) * P
                        mm = pe.transpose(turn[q % 2][:, b * P:(b + 1) * P], probs[:, col:col + P], ident[:, :])
                    mm.then_inc(turned, 1)

                turns(0)
                for q in range(len(widths)):
                    if q + 1 < len(widths):
                        turns(q + 1)
                    pe.wait_ge(copied, count + q + 1)
                    for b in range(widths[q]):
                        mm = pe.matmul(dst, pt_sb[:, q % 2, b * P:(b + 1) * P], rhs(4 * q + b),
                                       start=(q + b == 0), stop=(q == len(widths) - 1 and b == widths[q] - 1))
                return mm

            def one_round(st):
                g, k, r, t = st["graph"], st["pick"], st["fetch"], st["attend"]

                def step(s):
                    if r is not None:
                        fetch_group(r, s, 0)
                    if t is not None:
                        n = STEPS * t + s
                        after(pe, y_used, n)
                        pe.wait_ge(wq_in, 16 * (n + 1))
                        for e in range(2):
                            mm = pe.matmul(turn[0][:, e * P:(e + 1) * P], wq_pair[:, e * P:(e + 1) * P],
                                           xn1T[:, ds(t, 1), :], start=True, stop=True)
                        mm.then_inc(q_made, 1)
                    if g is not None:
                        for c in range(N // 512):
                            mm = pe.matmul(wide[:, c * 512:(c + 1) * 512], sel_head[:, ds(s, 1), :],
                                           dst3[:, c * 512:(c + 1) * 512], start=True, stop=True)
                        mm.then_inc(dst_shown, 1)
                    if k is not None:
                        pe.matmul(turn[1][:, :], xT_pick[:, :], mix_keys[:, ds(s * 512, 512)],
                                  start=True, stop=True).then_inc(sims_made, 1)
                    if t is not None:
                        width = sum(st["widths"]) * P
                        keys = lambda e, q, w: kv[:, 4 * q:4 * q + w, ds((2 * s + e) * P, P)]
                        values = lambda e: (lambda b: kv[:, b, ds((2 * s + e) * P + H * P, P)])

                        def s_rows(e):
                            for q, w in enumerate(st["widths"]):
                                mm = pe.matmul(wide[:, q * 512:q * 512 + w * P], qT[:, e, :], keys(e, q, w),
                                               start=True, stop=True)
                            mm.then_inc(s_made, 1)

                        pe.wait_ge(q_in, n + 1)
                        if g is not None:
                            pe.wait_ge(dst_used, STEPS * g + s + 1)
                        s_rows(0)
                    if k is not None:
                        pe.wait_ge(sims_in, STEPS * k + s + 1)
                    if g is not None:
                        m = STEPS * g + s
                        pe.wait_ge(gat_exp, m + 1)
                        after(pe, gat_out, m)
                        turn_and_sum(masked_dst, [4] * (N // 512), gat_turned, gat_copied, m * (N // 512),
                                     lambda b: h_all[:, ds(s * GD + b * P, GD)],
                                     acc[:, 256:256 + GD]).then_inc(gat_summed, 1)
                    if r is not None:
                        fetch_group(r, s, 1)
                    if t is not None:
                        chunks = st["chunks"] + 2 * len(st["widths"]) * s
                        pe.wait_ge(p_made, 2 * n + 1)
                        s_rows(1)
                        if g is not None:
                            pe.wait_ge(gat_out, m + 1)
                        after(pe, o_in, n)
                        turn_and_sum(att_p, st["widths"], p_turned, p_copied, chunks, values(0), acc[:, 0:P])
                    if r is not None:
                        fetch_group(r, s, 2)
                    if t is not None:
                        pe.wait_ge(p_made, 2 * n + 2)
                        turn_and_sum(att_p, st["widths"], p_turned, p_copied, chunks + len(st["widths"]), values(1),
                                     acc[:, P:2 * P]).then_inc(o_made, 1)
                    if r is not None:
                        fetch_group(r, s, 3)
                    if t is not None:
                        pe.wait_ge(o_in, n + 1)
                        for e in range(2):
                            mm = pe.transpose(turn[0][:, e * P:(e + 1) * P], o_sb[:, e, :], ident[:, :])
                        mm.then_inc(oT_made, 1)
                        pe.wait_ge(oT_in, n + 1)
                        pe.wait_ge(wo_in, 16 * (n + 1))
                        for e in range(2):
                            mm = pe.matmul(turn[1][:, 0:P], oT_sb[:, e, :], wo_pair[:, e, :],
                                           start=(e == 0), stop=(e == 1))
                        mm.then_inc(y_made, 1)

                if t is not None:
                    wait_alone(pe, k_kept, t + 1)
                    wait_alone(pe, v_kept, t + 1)
                with pe.Fori(0, STEPS) as s:
                    step(s)
                if k is not None:
                    pe.wait_ge(codes_ready, k + 1)
                    if t is not None:
                        pe.wait_ge(y_used, STEPS * (t + 1))
                    pe.transpose(turn[1][:, 0:P], w_tile[:, :], ident[:, :])
                    pe.transpose(turn[1][:, P:2 * P], code_tile[:, :], ident[:, :]).then_inc(codes_turned, 1)
                if r is not None:
                    pe.wait_ge(rows_out, STEPS * GROUPS * (r + 1))
                    for h in range(H):
                        mm = pe.transpose(wide[:, h * P:(h + 1) * P], stage[:, 1, h, :], ident[:, :])
                    mm.then_inc(v_turned, 1)
                if g is not None:
                    pe.wait_ge(xn1_made, g + 1)
                    pe.transpose(turn[0][:, 0:P], xn_tmp[:, :], ident[:, :]).then_inc(xn1T_made, 1)
                if k is not None:
                    pe.wait_ge(idx_ready, k + 1)
                if r is not None:
                    pe.wait_ge(v_kept, r + 1)
                if g is not None:
                    pe.wait_ge(xn1T_in, g + 1)

            every_round(pe, one_round)
            tail_tensor(pe, turn_and_sum)

        @block.scalar
        def _(act):
            act.wait_ge(c_mix, 1)
            act.activation(mix_keys[:, :], wide[:, :], ACT.Copy).then_inc(c_mix_sb, 1)
            act.wait_ge(c_xT, 1)
            act.activation(xnT_all, wide[:, 0:N], ACT.Copy).then_inc(c_xT_sb, 1)
            act.wait_ge(c_h, 1)
            act.activation(h_all, wide[:, 0:N], ACT.Copy).then_inc(c_h_sb, 1)
            act.wait_ge(c_d3, 1)
            for i in range(T // 8):
                last = act.activation(dst3[:, i * 1024:(i + 1) * 1024], turnb[i][0:96, :], ACT.Copy)
            last.then_inc(c_d3_sb, 1)

            def copy_chunks(widths, turned, copied, count):
                for q, w in enumerate(widths):
                    act.wait_ge(turned, count + q + 1)
                    act.activation(pt_sb[:, q % 2, 0:w * P], turn[q % 2][:, 0:w * P], ACT.Copy).then_inc(copied, 1)

            def fetch_out(r, s, j):
                act.wait_ge(rows_used, 2 + GROUPS * (STEPS * r + s) + j + 1)
                after(act, k_kept, r)
                act.activation(
                    stage[:, :, :, ds(s * TOK + j * GROUP, GROUP)],
                    rowsum[:, 0:P].rearrange("p (v k h) -> p v h k", v=2, h=H), ACT.Copy).then_inc(rows_out, 1)

            def one_round(st):
                g, k, r, t = st["graph"], st["pick"], st["fetch"], st["attend"]

                def step(s):
                    if r is not None:
                        fetch_out(r, s, 0)
                    if t is not None:
                        n = STEPS * t + s
                        act.wait_ge(q_made, n + 1)
                        act.activation(qT[:, :, :], turn[0][:, 0:2 * P].rearrange("p (e n) -> p e n", e=2), ACT.Copy,
                                       scale=float(P) ** -0.5).then_inc(q_in, 1)
                    if k is not None:
                        m = STEPS * k + s
                        act.wait_ge(sims_made, m + 1)
                        after(act, picks_done, m)
                        act.activation(sims[:, :, :], turn[1][:, :].rearrange("p (c n) -> p c n", c=4), ACT.Copy)\
                           .then_inc(sims_in, 1)
                    if g is not None:
                        m = STEPS * g + s
                        act.wait_ge(gat_logit, m + 1)
                        act.activation(masked_dst, masked_dst, ACT.Exp, bias=gs[:, 4:5], scale=SLOPE,
                                       accum_out=gat_sum[:, :]).then_inc(gat_exp, 1)
                        copy_chunks([4] * (N // 512), gat_turned, gat_copied, m * (N // 512))
                    if r is not None:
                        fetch_out(r, s, 1)
                    if t is not None:
                        width = sum(st["widths"]) * P
                        chunks = st["chunks"] + 2 * len(st["widths"]) * s
                        for e in range(2):
                            act.wait_ge(s_max, 2 * n + e + 1)
                            after(act, p_turned, chunks + e * len(st["widths"]))
                            act.activation(att_p[:, 0:width], wide[:, 0:width], ACT.Exp, bias=att_nm[:, e:e + 1],
                                           accum_out=att_sum[:, e:e + 1]).then_inc(p_made, 1)
                            copy_chunks(st["widths"], p_turned, p_copied, chunks + e * len(st["widths"]))
                            if e == 0 and r is not None:
                                fetch_out(r, s, 2)
                    elif r is not None:
                        fetch_out(r, s, 2)
                    if k is not None:
                        act.wait_ge(top_ready, STEPS * k + s + 1)
                        act.activation(top_e[:, :, :], top_d[:, :, :], ACT.Exp).then_inc(top_exp, 1)
                    if r is not None:
                        fetch_out(r, s, 3)
                    if t is not None:
                        act.wait_ge(oT_made, n + 1)
                        act.activation(oT_sb[:, :, :], turn[0][:, 0:2 * P].rearrange("p (e n) -> p e n", e=2),
                                       ACT.Copy).then_inc(oT_in, 1)

                with act.Fori(0, STEPS) as s:
                    step(s)
                if r is not None:
                    if isinstance(r, int) and r == 0:
                        act.wait_ge(c_zero, 1)
                    act.wait_ge(v_turned, r + 1)
                    act.activation(kv[:, ds(r, 1), H * P:2 * H * P], wide[:, 0:H * P].rearrange("p (o n) -> p o n", o=1),
                                   ACT.Copy).then_inc(v_kept, 1)
                if g is not None:
                    act.wait_ge(xn1T_made, g + 1)
                    act.activation(xT_pick[:, :], turn[0][:, 0:P], ACT.Copy)
                    act.activation(xn1T[:, ds(g, 1), :], turn[0][:, 0:P].rearrange("p (o n) -> p o n", o=1), ACT.Copy)\
                       .then_inc(xn1T_in, 1)

            every_round(act, one_round)
            tail_scalar(act, copy_chunks)

        @block.vector
        def _(dve):
            def inverse_root(var, n):
                v, y, q, z = (rs[:, i, 0:n] for i in range(4))
                dve.tensor_scalar(v, var, EPS, None, ALU.add)
                dve.drain()
                dve.tensor_scalar(rs_i[:, 0, 0:n], v.bitcast(I32), 1, None, ALU.logical_shift_right)
                dve.drain()
                dve.tensor_scalar(y.bitcast(I32), rs_i[:, 0, 0:n], -1.0, float(0x5F3759DF), ALU.mult, ALU.add)
                dve.drain()
                for _ in range(4):
                    dve.tensor_tensor(q, y, y, ALU.mult)
                    dve.drain()
                    dve.tensor_tensor(z, q, v, ALU.mult)
                    dve.drain()
                    dve.tensor_scalar(q, z, -0.5, 1.5, ALU.mult, ALU.add)
                    dve.drain()
                    dve.tensor_tensor(y, y, q, ALU.mult)
                    dve.drain()
                return y

            def norm(dst, src):
                dve.bn_stats(stats[:, 0, :], src)
                dve.drain()
                dve.bn_aggr(moments[:, 0, :], stats[:, 0, :])
                dve.drain()
                y = inverse_root(moments[:, 0, 1:2], 1)
                return dve.tensor_scalar(dst, src, moments[:, 0, 0:1], y, ALU.subtract, ALU.mult)

            dve.memset(dst_nat[:, 0:768], 0.0)
            dve.memset(dst_nat2[:, 0:768], 0.0)
            dve.wait_ge(c_ab, 64)
            dve.wait_ge(c_ident, 1)
            for side in range(2):
                last = dve.tensor_scalar(a_block[:, side * GH:(side + 1) * GH], col_head[:, :], a_col[:, side:side + 1],
                                         None, ALU.mult)
            last.then_inc(c_ablock, 1)
            dve.wait_ge(c_x, 16)
            for t in range(T):
                dve.bn_stats(stats[:, t, :], x_all[:, t, :])
            dve.drain()
            for t in range(T):
                dve.bn_aggr(moments[:, t, :], stats[:, t, :])
            dve.drain()
            y = inverse_root(moments[:, :, 1], T)
            for t in range(T):
                last = dve.tensor_scalar(x_all[:, t, :], x_all[:, t, :], moments[:, t, 0:1], y[:, t:t + 1],
                                         ALU.subtract, ALU.mult)
            last.then_inc(c_xn, 1)
            dve.wait_ge(c_wa, 1)
            dve.tensor_copy(wa[:, :], acc[:, 0:2 * GH]).then_inc(c_wa_sb, 1)
            dve.wait_ge(c_adj, 16)
            dve.tensor_scalar(edge_hide, masked_dst, 0.0, HIDE, ALU.is_le, ALU.mult)
            dve.wait_ge(c_sd, 1)
            dve.tensor_copy(src_dst[:, :, :], acc[:, 0:8 * T].rearrange("p (t c) -> p t c", c=8))
            dve.drain()
            left = dst_parts[:, 0:T * GH].rearrange("p (t h) -> p t h", h=GH)
            dve.tensor_copy(left, src_dst[:, :, GH:2 * GH])
            dve.drain()
            for part in range(3):
                for half in range(T // 8):
                    nat = (dst_nat, dst_nat2)[half][:, 0:768].rearrange("p (t c) -> p t c", c=96)
                    last = dve.tensor_copy(nat[:, :, 32 * part:32 * part + GH], left[:, half * 8:half * 8 + 8, :])
                dve.drain()
                if part < 2:
                    for half in range(T // 8):
                        nat = (dst_nat, dst_nat2)[half][:, 0:768].rearrange("p (t c) -> p t c", c=96)
                        rest = left[:, half * 8:half * 8 + 8, :]
                        dve.tensor_tensor(rest, rest, nat[:, :, 32 * part:32 * part + GH], ALU.subtract)
                    dve.drain()
            dve.sem_inc(c_sd_sb, 1)
            dve.wait_ge(c_mem, 64)
            dve.wait_ge(c_d3, 1)

            def weight_block(n):
                w = wT[:, :, :].rearrange("p b n -> p (b n)")[:, ds((n * TOK) % (2 * P), TOK)]
                dve.tensor_tensor(w_block[:, ds(n % 2, 1), :, :].rearrange("p o t h -> p (o t) h"),
                                  w.rearrange("p (t o) -> p t o", o=1).to_broadcast([P, TOK, H]),
                                  row_head[:, :].rearrange("p (o h) -> p o h", o=1).to_broadcast([P, TOK, H]),
                                  ALU.mult).then_inc(wblock_ready, 1)

            def graph_logits(g, s):
                m = STEPS * g + s
                dve.tensor_copy(src_now[:, :], src_dst[:, ds(g, 1), ds(s, 1)].rearrange("p a b -> p (a b)"))
                wait_alone(dve, dst_shown, m + 1)
                if not isinstance(m, int) or m > 0:
                    wait_alone(dve, gat_summed, m)
                dve.tensor_tensor_reduce(masked_dst, wide[:, 0:N], edge_hide, 1.0, -3e38, ALU.add, ALU.max,
                                         gs[:, 0:1]).then_inc(dst_used, 1)
                dve.drain()
                dve.tensor_scalar(gs[:, 1:2], gs[:, 0:1], src_now[:, :], None, ALU.add)
                dve.tensor_scalar(gs[:, 3:4], src_now[:, :], SLOPE, None, ALU.mult)
                dve.drain()
                dve.scalar_tensor_tensor(gs[:, 2:3], gs[:, 1:2], SLOPE, gs[:, 1:2], ALU.mult, ALU.max)
                dve.drain()
                dve.tensor_tensor(gs[:, 4:5], gs[:, 3:4], gs[:, 2:3], ALU.subtract)
                for c in range(N // 512):
                    part = masked_dst[:, c * 512:(c + 1) * 512]
                    dve.tensor_scalar(scratch[:, :], part, src_now[:, :], 0.0, ALU.add, ALU.max)
                    dve.drain()
                    last = dve.scalar_tensor_tensor(part, scratch[:, :], 4.0, part, ALU.mult, ALU.add)
                    dve.drain()
                last.then_inc(gat_logit, 1)

            def graph_head_out(g, s):
                m = STEPS * g + s
                dve.wait_ge(gat_exp, m + 1)
                dve.reciprocal(gs[:, 5:6], gat_sum[:, :])
                dve.drain()
                dve.wait_ge(gat_summed, m + 1)
                dve.tensor_scalar(g_out[:, ds(s * GD, GD)], acc[:, 256:256 + GD], gs[:, 5:6], None, ALU.mult)\
                   .then_inc(gat_out, 1)

            def row_max(st, s, e):
                width = sum(st["widths"]) * P
                wait_alone(dve, s_made, 2 * (STEPS * st["attend"] + s) + e + 1)
                if st["whole"]:
                    part, mask = wide[:, width - 512:width], mask_wide[:, ds((3 - st["i"]) * P, 512)]
                else:
                    part, mask = wide[:, width - P:width], mask_wide[:, 384:512]
                dve.tensor_tensor(part, part, mask, ALU.add)
                dve.drain()
                dve.reduce_max(att_m[:, e:e + 1], wide[:, 0:width], AX)
                dve.drain()
                dve.tensor_scalar(att_nm[:, e:e + 1], att_m[:, e:e + 1], -1.0, None, ALU.mult).then_inc(s_max, 1)

            def pick_keys(k, s):
                wait_alone(dve, sims_in, STEPS * k + s + 1)
                sides = [(e, p) for e in range(2) for p in range(2)]
                left = lambda e, p: scratch[:, (2 * e + p) * P:(2 * e + p + 1) * P]
                for e, p in sides:
                    dve.max(best[:, e, p, 0:8], sims[:, 2 * e + p, :])
                dve.drain()
                for e, p in sides:
                    dve.match_replace(left(e, p), best[:, e, p, 0:8], sims[:, 2 * e + p, :], -3e38)
                for e, p in sides:
                    dve.max_index(place[:, e, p, 0:8], best[:, e, p, 0:8], sims[:, 2 * e + p, :])
                dve.drain()
                for e, p in sides:
                    dve.max(best[:, e, p, 8:16], left(e, p))
                dve.drain()
                for e, p in sides:
                    dve.max_index(place[:, e, p, 8:16], best[:, e, p, 8:16], left(e, p))
                for e in range(2):
                    dve.tensor_tensor(
                        cand[:, e, :].rearrange("p (i j) -> p i j", j=K),
                        best[:, e, 0, :].rearrange("p (i o) -> p i o", o=1).to_broadcast([P, K, K]),
                        best[:, e, 1, :].rearrange("p (o j) -> p o j", o=1).to_broadcast([P, K, K]), ALU.add)
                dve.drain()
                dve.tensor_copy(placef[:, :, :, :], place[:, :, :, :])

            def pick_pairs(k, s):
                rest = lambda e: sims[:, 2 * e:2 * e + 2, :].rearrange("p a n -> p (a n)")
                for e in range(2):
                    dve.max(top[:, e, 0:8], cand[:, e, :])
                dve.drain()
                for e in range(2):
                    dve.match_replace(rest(e), top[:, e, 0:8], cand[:, e, :], -3e38)
                for e in range(2):
                    dve.max_index(pos[:, e, 0:8], top[:, e, 0:8], cand[:, e, :])
                dve.drain()
                for e in range(2):
                    dve.max(top[:, e, 8:16], rest(e))
                dve.drain()
                for e in range(2):
                    last = dve.max_index(pos[:, e, 8:16], top[:, e, 8:16], rest(e))
                last.then_inc(picks_done, 1)
                dve.tensor_tensor(top_d[:, :, :], top[:, :, :], top[:, :, 0:1].to_broadcast([P, 2, K]),
                                  ALU.subtract).then_inc(top_ready, 1)
                dve.drain()
                dve.tensor_scalar(pos_hi[:, :, :], pos[:, :, :], 4, None, ALU.logical_shift_right)
                dve.tensor_scalar(pos_lo[:, :, :], pos[:, :, :], K - 1, None, ALU.bitwise_and)
                dve.drain()
                for side, (where, key) in enumerate(((pos_hi, key0), (pos_lo, key1))):
                    hit = scratch[:, :].rearrange("p (n j) -> p n j", j=K)
                    dve.tensor_tensor(
                        hit, where[:, :, :].rearrange("p e (n o) -> p (e n) o", o=1).to_broadcast([P, 2 * K, K]),
                        iota16[:, :].rearrange("p (o j) -> p o j", o=1).to_broadcast([P, 2 * K, K]), ALU.is_equal)
                    dve.drain()
                    hit4 = scratch[:, :].rearrange("p (e n j) -> p e n j", e=2, j=K)
                    dve.tensor_tensor(
                        hit4, hit4,
                        placef[:, :, side, :].rearrange("p e (o j) -> p e o j", o=1).to_broadcast([P, 2, K, K]),
                        ALU.mult)
                    dve.drain()
                    dve.reduce_sum(key[:, :, :].rearrange("p e n -> p (e n)"), hit, AX)
                    dve.drain()
                dve.scalar_tensor_tensor(code_tile[:, ds(s * 2 * K, 2 * K)],
                                         key1[:, :, :].rearrange("p e n -> p (e n)"), float(P),
                                         key0[:, :, :].rearrange("p e n -> p (e n)"), ALU.mult, ALU.add)

            def pick_weights(k, s):
                dve.wait_ge(top_exp, STEPS * k + s + 1)
                dve.reduce_sum(top_s[:, 0, :], top_e[:, :, :], AX)
                dve.drain()
                dve.reciprocal(top_s[:, 1, :], top_s[:, 0, :])
                dve.drain()
                dve.tensor_tensor(w_tile[:, ds(s * 2 * K, 2 * K)].rearrange("p (e n) -> p e n", e=2), top_e[:, :, :],
                                  top_s[:, 1, :].rearrange("p (e o) -> p e o", o=1).to_broadcast([P, 2, K]), ALU.mult)

            def one_round(st):
                g, k, r, t = st["graph"], st["pick"], st["fetch"], st["attend"]
                if isinstance(r, int) and r == 0:
                    dve.drain()
                    weight_block(0)

                def step(s):
                    if g is not None:
                        graph_logits(g, s)
                    if t is not None:
                        row_max(st, s, 0)
                    if g is not None:
                        graph_head_out(g, s)
                    if k is not None:
                        pick_keys(k, s)
                    if t is not None:
                        row_max(st, s, 1)
                    if k is not None:
                        pick_pairs(k, s)
                    if r is not None:
                        n = STEPS * r + s
                        dve.wait_ge(rows_used, 2 + GROUPS * n)
                        weight_block(n + 1)
                    if k is not None:
                        pick_weights(k, s)
                    if t is not None:
                        n = STEPS * t + s
                        dve.wait_ge(p_made, 2 * n + 2)
                        dve.reciprocal(att_r[:, :], att_sum[:, :])
                        dve.drain()
                        dve.wait_ge(o_made, n + 1)
                        for e in range(2):
                            last = dve.tensor_scalar(o_sb[:, e, :], acc[:, e * P:(e + 1) * P], att_r[:, e:e + 1], None,
                                                     ALU.mult)
                        last.then_inc(o_in, 1)
                        dve.wait_ge(y_made, n + 1)
                        dve.wait_ge(x1_back, 16 * (t + 1))
                        dve.tensor_tensor(y_acc[:, :], y_acc[:, :], turn[1][:, 0:P], ALU.add).then_inc(y_used, 1)
                        dve.drain()

                with dve.Fori(0, STEPS) as s:
                    step(s)
                if k is not None:
                    dve.drain()
                    dve.tensor_tensor(code_tile[:, :], code_tile[:, :], head_base[:, :], ALU.add).then_inc(codes_ready, 1)
                if g is not None:
                    dve.drain()
                    norm(ln_tmp[:, :], g_out[:, :])
                    dve.drain()
                    dve.tensor_tensor(ln_tmp[:, :], ln_tmp[:, :], gamma_b[:, :], ALU.mult)
                    dve.wait_ge(xt_in, 16 * (g + 1))
                    dve.tensor_tensor(xn_tmp[:, :], xt[:, :], beta_b[:, :], ALU.add)
                    dve.drain()
                    after(dve, x1_out, 16 * g)
                    dve.tensor_tensor(x1[:, :], ln_tmp[:, :], xn_tmp[:, :], ALU.add).then_inc(x1_made, 1)
                    dve.drain()
                    norm(xn_tmp[:, :], x1[:, :]).then_inc(xn1_made, 1)
                if k is not None:
                    dve.wait_ge(codes_turned, k + 1)
                    after(dve, idx_copied, 2 * STEPS * (k - 1))
                    dve.tensor_copy(wT[:, ds(k % 2, 1), :], turn[1][:, 0:P].rearrange("p (o n) -> p o n", o=1))
                    dve.tensor_copy(idxT[:, ds(k % 2, 1), :], turn[1][:, P:2 * P].rearrange("p (o n) -> p o n", o=1))\
                       .then_inc(idx_ready, 1)
                if r is not None:
                    if isinstance(r, int) and r == 0:
                        dve.wait_ge(c_zero, 1)
                    dve.wait_ge(v_turned, r + 1)
                    dve.tensor_copy(kv[:, ds(r, 1), 0:H * P], stage[:, 0, :, :].rearrange("p (o h) n -> p o (h n)", o=1))\
                       .then_inc(k_kept, 1)
                if t is not None:
                    dve.sem_inc(x2_made, 1)
                    norm(o_sb[:, 0, :], y_acc[:, :])
                    dve.drain()
                    dve.tensor_tensor(ln_tmp[:, :], o_sb[:, 0, :], hv_b[:, :], ALU.mult)
                    dve.tensor_copy(xn1T[:, ds(t, 1), :], o_sb[:, 0, :].rearrange("p (o n) -> p o n", o=1))
                    dve.drain()
                    dve.reduce_sum(scores[:, ds(t, 1)], ln_tmp[:, :], AX).then_inc(xn2_made, 1)
                if g is not None:
                    dve.wait_ge(adj_in, 16 * (g + 1))
                    dve.tensor_scalar(edge_hide, masked_dst, 0.0, HIDE, ALU.is_le, ALU.mult)
                    dve.drain()

            every_round(dve, one_round)
            tail_vector(dve, inverse_root)


def kernel(x, adj, L0_gnn_W, L0_gnn_a, L0_gnn_gamma, L0_gnn_beta, L0_ffn_Wq_pk, L0_ffn_pk_keys, L0_ffn_Wq,
           L0_ffn_keys_table, L0_ffn_values_table, L0_ffn_Wo, L1_gnn_H_v, L1_ffn_router_w, L1_ffn_router_b,
           L1_ffn_W1, L1_ffn_b1, L1_ffn_W2, L1_ffn_b2):
    import numpy as np
    import concourse.bacc as bacc
    from concourse.bass_utils import run_bass_kernel_spmd

    D = L0_ffn_Wq_pk.shape[0]
    sides, keys, heads, dk = L0_ffn_pk_keys.shape
    E, _, hidden = L1_ffn_W1.shape
    lay = lambda v: np.ascontiguousarray(v)
    arrays = {
        "x": lay(x), "adj": lay(adj), "W": lay(L0_gnn_W), "WT": lay(np.transpose(L0_gnn_W)), "a": lay(np.transpose(np.reshape(L0_gnn_a, (2, -1)))),
        "gamma": lay(L0_gnn_gamma), "beta": lay(L0_gnn_beta),
        "WqpkT": lay(np.transpose(np.reshape(L0_ffn_Wq_pk, (D, sides, heads, dk)), (3, 2, 1, 0))).reshape(dk, -1),
        "pkT": lay(np.transpose(L0_ffn_pk_keys, (3, 2, 0, 1))).reshape(dk, -1),
        "Wq": lay(L0_ffn_Wq),
        "kv_table": np.concatenate([L0_ffn_keys_table, L0_ffn_values_table], axis=1),
        "Wo": lay(L0_ffn_Wo), "Hv": lay(L1_gnn_H_v),
        "router_wT": lay(np.transpose(L1_ffn_router_w)), "router_b": lay(L1_ffn_router_b),
        "W1": lay(np.transpose(L1_ffn_W1, (1, 0, 2))).reshape(D, E * hidden),
        "b1": lay(np.transpose(np.reshape(L1_ffn_b1, (-1, P)))),
        "W2": lay(np.reshape(L1_ffn_W2, (E * hidden, D))), "b2": lay(L1_ffn_b2),
    }
    nc = bacc.Bacc("TRN2", target_bir_lowering=False, num_devices=1)
    in_maps, args = {}, []
    for name, v in arrays.items():
        in_maps[f"in_{name}"] = v
        args.append(nc.dram_tensor(f"in_{name}", v.shape, mybir.dt.from_np(v.dtype), kind="ExternalInput").ap())
    args.append(nc.dram_tensor("out_0", x.shape, F32, kind="ExternalOutput").ap())
    build_network(nc, *args)
    r = run_bass_kernel_spmd(nc, [in_maps], core_ids=[0])
    return r.results[0]["out_0"]
```

```python
from contextlib import ExitStack

import concourse.bass as bass
from concourse import mybir
from concourse.alu_op_type import AluOpType as ALU

F32 = mybir.dt.float32
BF16 = mybir.dt.bfloat16
U32 = mybir.dt.uint32
I32 = mybir.dt.int32
ACT = mybir.ActivationFunctionType
AX = mybir.AxisListType.X
P = 128
EPS = 1e-5
HIDE = -1e30
ds = bass.ds


def plan_rounds(tiles):
    plan = [(r, 1) for r in range(-4, 0)]
    r = 0
    while r + 7 < tiles:
        plan.append((r, 4))
        r += 4
    return plan + [(q, 1) for q in range(r, tiles)]


def chunk_widths(first, rounds):
    blocks = first + rounds
    return [4] * (blocks // 4) + ([blocks % 4] if blocks % 4 else [])


def build_network(nc, x, adj, W, WT, a, gamma, beta, WqpkT, pkT, Wq, kv_table, Wo, Hv,
                  router_wT, router_b, W1, b1, W2, b2, out):
    N = x.shape[0]
    T = N // P
    GH, GD = 4, 32
    H, K = 8, 16
    E = router_wT.shape[1]
    EC = W1.shape[1] // P
    KEYS_PER_HEAD = kv_table.shape[0] // H
    ROW = kv_table.shape[1]
    STEPS = 4
    TOK = P // STEPS
    GROUP = 4
    GROUPS = TOK // GROUP
    SLOTS = 4
    PAIRS = GROUPS // 2
    SLOPE = 0.2
    plan = plan_rounds(T)

    starts_at = {}

    def at(sem, n):
        return n + starts_at.get(sem.name, 0)

    def after(eng, sem, n):
        if not isinstance(n, int) or n > 0:
            eng.wait_ge(sem, at(sem, n))

    def wait_alone(eng, sem, n):
        eng.wait_ge(sem, at(sem, n))
        eng.sem_inc(passed, 1)

    chunks_before = [0]
    for first, rounds in plan:
        if first >= 0:
            for _ in range(rounds):
                chunks_before.append(chunks_before[-1] + H * len(chunk_widths(first, rounds)))

    x1_dram = nc.dram_tensor("x1_dram", [N, P], F32, kind="Internal").ap()
    x2_dram = nc.dram_tensor("x2_dram", [N, P], F32, kind="Internal").ap()

    with ExitStack() as ctx:
        def sb(name, shape, dt=F32):
            return ctx.enter_context(nc.sbuf_tensor(name, shape, dt))

        def sem(name):
            return ctx.enter_context(nc.semaphore(name))

        TILE_KV = 2 * H * P
        kv = sb("kv", [P, T, TILE_KV])
        last3 = kv[:, T - 3:T, :].rearrange("p t n -> p (t n)")
        h_all = last3[:, 0:N]
        masked_dst = last3[:, 2048:2048 + N]
        edge_hide = last3[:, 4096:5120].bitcast(BF16)[:, 0:N]
        dst3 = last3[0:96, 5120:6144].bitcast(BF16)[:, 0:N]
        xnT_all = kv[:, T - 4, 0:N]
        stage = sb("stage", [P, 2, H, P])
        ring = sb("ring", [P, SLOTS, GROUP, ROW])
        mix_keys = sb("mix_keys", [P, 2048])
        xn1T = sb("xn1T", [P, T, P])
        att_p = sb("att_p", [P, max(N, 2048)])
        pt_sb = sb("pt_sb", [P, 2, 512])
        mask_wide = sb("mask_wide", [P, 896], BF16)
        wT = sb("wT", [P, 2, P])
        idxT = sb("idxT", [P, 2, P], U32)
        idx_now = sb("idx_now", [P, 2, SLOTS * GROUP], U32)
        w_block = sb("w_block", [P, 2, TOK // 2, H])
        sums_sb = sb("sums_sb", [P, 2 * ROW])
        sims = sb("sims", [P, 4, P])
        scratch = sb("scratch", [P, 512])
        cand = sb("cand", [P, 2, K * K])
        ident = sb("ident", [P, P])
        identb = sb("identb", [P, P], BF16)
        sel_head = sb("sel_head", [96, GH, P], BF16)
        gamma_b = sb("gamma_b", [P, P])
        beta_b = sb("beta_b", [P, P])
        hv_b = sb("hv_b", [P, P])
        wq_pair = sb("wq_pair", [P, 2 * P])
        wo_pair = sb("wo_pair", [P, 2, P])
        qT = sb("qT", [P, 2, P])
        o_sb = sb("o_sb", [P, 2, P])
        y_acc = sb("y_acc", [P, P])
        xt = sb("xt", [P, P])
        x1 = sb("x1", [P, P])
        g_out = sb("g_out", [P, P])
        xn_tmp = sb("xn_tmp", [P, P])
        xT_pick = sb("xT_pick", [P, P])
        w_tile = sb("w_tile", [P, P])
        code_tile = sb("code_tile", [P, P])
        head_base = sb("head_base", [P, P])
        best = sb("best", [P, 2, 2, K])
        place = sb("place", [P, 2, 2, K], U32)
        placef = sb("placef", [P, 2, 2, K])
        top = sb("top", [P, 2, K])
        pos = sb("pos", [P, 2, K], U32)
        pos_hi = sb("pos_hi", [P, 2, K], U32)
        pos_lo = sb("pos_lo", [P, 2, K], U32)
        key0 = sb("key0", [P, 2, K])
        key1 = sb("key1", [P, 2, K])
        top_d = sb("top_d", [P, 2, K])
        top_e = sb("top_e", [P, 2, K])
        top_s = sb("top_s", [P, 2, 2])
        iota16 = sb("iota16", [P, K])
        iota32 = sb("iota32", [P, E])
        row_head = sb("row_head", [P, H])
        col_head = sb("col_head", [P, GH])
        a_col = sb("a_col", [P, 2])
        a_block = sb("a_block", [P, 2 * GH])
        wa = sb("wa", [P, 2 * GH])
        src_dst = sb("src_dst", [P, T, 2 * GH])
        src_now = sb("src_now", [P, 1])
        gs = sb("gs", [P, 8])
        gat_sum = sb("gat_sum", [P, 1])
        att_m = sb("att_m", [P, 2])
        att_nm = sb("att_nm", [P, 2])
        att_sum = sb("att_sum", [P, 2])
        att_r = sb("att_r", [P, 2])
        stats = sb("stats", [P, T, 6])
        moments = sb("moments", [P, T, 2])
        rs = sb("rs", [P, 4, T])
        rs_i = sb("rs_i", [P, 2, T], I32)
        scores = sb("scores", [P, T])
        mix_m = sb("mix_m", [P, 4])
        mix_nm = sb("mix_nm", [P, 4])
        mix_any = sb("mix_any", [P, 4])
        mix_sum = sb("mix_sum", [P, 4])
        mix_r = sb("mix_r", [P, 4])
        oT_sb = qT
        ln_tmp = scratch[:, 0:P]
        x_all = ring[:, :, :, :].rearrange("p s g n -> p (s g n)")[:, 0:N].rearrange("p (t d) -> p t d", d=P)
        wqpkT_sb = stage[0:64, :, :, :].rearrange("p k h n -> p (k h n)")
        pkT_sb = att_p[0:64, 0:2048]
        wt_sb = g_out
        gat_w = xn_tmp
        iota_i = cand[:, 0, 0:P].bitcast(I32)
        dst_parts = w_block[:, :, :, :].rearrange("p b t h -> p (b t h)")
        dst_nat = sims[:, :, :].rearrange("p a n -> p (a n)").bitcast(BF16)
        dst_nat2 = scratch[:, :].bitcast(BF16)
        free = kv[:, :, :].rearrange("p t n -> p (t n)")
        adj_sb = free[:, 0:4096].rearrange("p (b n) -> p b n", b=2)
        logit = free[:, 4096:8192].rearrange("p (b n) -> p b n", b=2)
        score_b = free[:, 8192:8192 + N]
        hid = free[:, 10240:10240 + EC * 512].rearrange("p (c n) -> p c n", c=EC)
        w1_sb = mix_keys[:, 0:E * 32]
        w2_sb = mix_keys[:, 1024:2048].rearrange("p (c n) -> p c n", c=EC)
        b1_sb = sb("b1_sb", [P, EC])
        b2_sb = xt[0:E, :]
        rw_sb = code_tile[:, 0:E]
        rb_sb = code_tile[:, E:2 * E]
        sel_expert = cand[0:E, :, :].rearrange("p a n -> p (a n)").bitcast(BF16).rearrange("p (c n) -> p c n", c=EC)
        x3 = stage[:, 0, 0:4, :]
        y_moe = stage[:, 0, 4:8, :]
        xn3T = stage[:, 1, 0:4, :]
        x2_in = stage[:, 1, 4:8, :]
        onehotT = scratch[0:E, :]
        onehotTb = sims[0:E, :, :].rearrange("p a n -> p (a n)").bitcast(BF16)[:, 0:512]
        xn3 = free[:, 10240:10752].rearrange("p (j n) -> p j n", j=4)
        onehot = w_tile[:, :].rearrange("p (j e) -> p j e", j=4)
        rlog = ln_tmp[:, :].rearrange("p (j e) -> p j e", j=4)
        rtop = best[:, :, :, :].rearrange("p a b k -> p (a b k)")[:, 0:32].rearrange("p (j k) -> p j k", j=4)
        rpos = place[:, :, :, :].rearrange("p a b k -> p (a b k)")[:, 0:32].rearrange("p (j k) -> p j k", j=4)
        rposf = placef[:, :, :, :].rearrange("p a b k -> p (a b k)")[:, 0:32].rearrange("p (j k) -> p j k", j=4)

        wide = ctx.enter_context(nc.psum_tensor("wide", [P, 2048], F32))
        turn = [ctx.enter_context(nc.psum_tensor(f"turn{i}", [P, 512], F32)) for i in range(2)]
        rowsum = ctx.enter_context(nc.psum_tensor("rowsum", [P, 512], F32))
        acc = ctx.enter_context(nc.psum_tensor("acc", [P, 512], F32))
        turnb = [t[:, :].bitcast(BF16) for t in turn]

        (c_mem, c_ln, c_x, c_w, c_pk, c_ab, c_ablock, c_adj, c_ident, c_wa_in, c_wa, c_wa_sb, c_mix, c_mix_sb, c_xn, c_xT,
         c_xT_sb, c_h, c_sd, c_h_sb, c_sd_sb, c_d3, c_d3_sb, c_hide, c_pool, c_zero) = [
            sem("start_" + n) for n in
            "mem ln x w pk ab ablock adj ident wa_in wa wa_sb mix mix_sb xn xT xT_sb h sd h_sb sd_sb d3 d3_sb hide pool zero".split()]
        dst_shown, dst_used, gat_bent, gat_logit, gat_exp, gat_turned, gat_copied, gat_summed, gat_out = [
            sem("gat_" + n) for n in "shown used bent logit exp turned copied summed out".split()]
        sims_made, sims_in, picks_done, top_ready, top_exp = [
            sem("pick_" + n) for n in "made in done top exp".split()]
        codes_ready, codes_turned, idx_ready, idx_copied, idx_staged = [
            sem("code_" + n) for n in "ready turned idx copied staged".split()]
        row_in = [sem(f"row_in{i}") for i in range(SLOTS)]
        rows_used, rows_copied, rows_turned, rows_out, wblock_ready = [
            sem("rows_" + n) for n in "used copied turned out wblock".split()]
        v_turned, v_kept, k_kept = [sem("kv_" + n) for n in "vturned vkept kkept".split()]
        wq_in, wo_in, q_made, q_in, s_made, s_max, p_made, p_turned, p_copied, o_made, o_in, oT_made, oT_in, y_made, \
            y_used = [sem("att_" + n) for n in
                      "wqin woin qmade qin smade smax p turned copied omade oin oTmade oTin ymade yused".split()]
        xt_in, adj_in, hide_ready, x1_made, x1_out, xn1_made, xn1T_made, xn1T_in = [
            sem("mid_" + n) for n in "xt adj hide x1 x1out xn1 xn1T xn1Tin".split()]
        t_w, t_sel, t_x2, t_adj0, t_adj1, t_out, y_free = [
            sem("last_" + n) for n in "w sel x2 adj0 adj1 out yfree".split()]
        score_rows, score_shown, score_in, mix_logit, mix_exp, mix_turned, mix_copied, mix_summed, x3_made = [
            sem("mix_" + n) for n in "rows shown in logit exp turned copied summed x3".split()]
        xn3_made, xn3T_made, xn3T_in, route_made, route_hot, hot_turned, hot_in, hid_made, hid_relu, hid_masked, \
            moe_made, moe_relu, moe_out = [sem("moe_" + n) for n in
            "xn3 xn3T xn3Tin route hot turned in hid relu masked made relu2 out".split()]
        t_adj = [t_adj0, t_adj1]
        passed = sem("passed")
        x1_back, x2_made, x2_out, xn2_made = [sem("end_" + n) for n in "x1back x2 x2out xn2".split()]

        starts = [(rows_used, 2 * SLOTS), (rows_out, 1), (mix_logit, 2), (x3_made, 2), (hid_masked, 2)] + [
            (free_, 1) for free_ in (x1_made, x2_out, xn2_made, q_made, y_made, gat_summed, y_used, gat_out, o_in,
                                     picks_done, p_turned, k_kept, x1_out, idx_copied, y_free)]
        starts_at.update({free_.name: n for free_, n in starts})

        def stages(first, rounds, i):
            t = first + i
            has = lambda off: 0 <= first + off and first + rounds - 1 + off < T
            return {
                "graph": t + 4 if has(4) else None,
                "pick": t + 3 if has(3) else None,
                "fetch": t + 1 if has(1) else None,
                "attend": t if has(0) else None,
                "widths": chunk_widths(first, rounds) if has(0) else None,
                "chunks": (chunks_before[first] + (H * len(chunk_widths(first, rounds))) * i) if has(0) else None,
                "whole": rounds > 1,
                "i": i,
            }

        def every_round(eng, body):
            for first, rounds in plan:
                if rounds == 1:
                    body(stages(first, rounds, 0))
                else:
                    with eng.Fori(0, rounds) as i:
                        body(stages(first, rounds, i))

        def tail_sync(sp):
            sp.wait_ge(sims_made, STEPS * T)
            sp.dma_start(w1_sb, W1).then_inc(t_w, 16)
            sp.dma_start(w2_sb, W2.rearrange("(c p) n -> p c n", p=P)).then_inc(t_w, 16)
            sp.wait_ge(codes_turned, T)
            sp.dma_start(rw_sb, router_wT).then_inc(t_w, 16)
            sp.dma_start(rb_sb, router_b.partition_broadcast(P)).then_inc(t_w, 16)
            sp.wait_ge(x1_made, at(x1_made, T))
            sp.dma_start(b2_sb, b2).then_inc(t_w, 16)
            sp.wait_ge(xn2_made, at(xn2_made, T))
            sp.wait_ge(x2_out, at(x2_out, 16 * T))
            with sp.Fori(0, T // 4) as u:
                sp.wait_ge(x3_made, at(x3_made, 4 * u))
                sp.dma_start(x2_in, x2_dram.rearrange("(t p) d -> p t d", p=P)[:, ds(4 * u, 4), :]).then_inc(t_x2, 16)
                for j in range(4):
                    i = 4 * u + j
                    sp.wait_ge(mix_logit, at(mix_logit, i - 1))
                    sp.dma_start(adj_sb[:, j % 2, 0:N], adj[ds(i * P, P), :]).then_inc(t_adj[j % 2], 16)

        def tail_pool(pool):
            pool.wait_ge(picks_done, at(picks_done, STEPS * T))
            pool.memset(sel_expert, 0.0).then_inc(c_pool, 1)
            pool.wait_ge(c_pool, 4)
            pool.affine_select(out=sel_expert.rearrange("e c (q n) -> e c q n", q=4),
                               in_=sel_expert.rearrange("e c (q n) -> e c q n", q=4),
                               compare_op=ALU.not_equal, fill=1.0, base=0,
                               pattern=[[-4, EC], [-1, 4], [0, 32]], channel_multiplier=1).then_inc(t_sel, 1)
            with pool.Fori(0, T // 4) as u:
                pool.wait_ge(moe_out, u + 1)
                pool.dma_start(out.rearrange("(t p) d -> p t d", p=P)[:, ds(4 * u, 4), :], y_moe).then_inc(t_out, 16)
                pool.wait_ge(t_out, 16 * (u + 1))
                pool.sem_inc(y_free, 1)

        def tail_tensor(pe, turn_and_sum):
            pe.wait_ge(score_rows, 1)
            for t in range(T):
                mm = pe.matmul(wide[:, t * P:(t + 1) * P], att_p[:, t * P:(t + 1) * P], ident[:, :],
                               start=True, stop=True)
            mm.then_inc(score_shown, 1)
            pe.wait_ge(score_in, 1)
            pe.wait_ge(t_w, 16 * 5)
            pe.wait_ge(t_sel, 1)
            with pe.Fori(0, T // 4) as u:
                for j in range(4):
                    i = 4 * u + j
                    pe.wait_ge(mix_exp, i + 1)
                    pe.wait_ge(x3_made, at(x3_made, i - 1))
                    turn_and_sum(logit[:, j % 2, :], [4] * (N // 512), mix_turned, mix_copied, i * (N // 512),
                                 lambda b: xn1T[:, b, :], (acc, rowsum)[j % 2][:, 0:P]).then_inc(mix_summed, 1)
                pe.wait_ge(xn3_made, u + 1)
                for j in range(4):
                    mm = pe.transpose(turn[0][:, j * P:(j + 1) * P], xn3[:, j, :], ident[:, :])
                mm.then_inc(xn3T_made, 1)
                pe.wait_ge(xn3T_in, u + 1)
                for j in range(4):
                    mm = pe.matmul(turn[1][:, j * E:(j + 1) * E], xn3T[:, j, :], rw_sb, start=True, stop=True)
                mm.then_inc(route_made, 1)
                pe.wait_ge(route_hot, u + 1)
                for j in range(4):
                    mm = pe.transpose(turn[0][0:E, j * P:(j + 1) * P], onehot[:, j, :], ident[:, :])
                mm.then_inc(hot_turned, 1)
                pe.wait_ge(hot_in, u + 1)
                for c in range(EC):
                    pe.wait_ge(hid_masked, at(hid_masked, EC * u + c - 1))
                    b = c % 2
                    pe.matmul(wide[:, b * 512:(b + 1) * 512], w1_sb[:, c * P:(c + 1) * P],
                              xn3T.rearrange("p j n -> p (j n)"), start=True, stop=True)
                    pe.matmul(wide[:, 1024 + b * 512:1536 + b * 512], sel_expert[:, c, :], onehotTb,
                              start=True, stop=True).then_inc(hid_made, 1)
                pe.wait_ge(hid_masked, at(hid_masked, EC * (u + 1)))
                for j in range(4):
                    dst = turn[1][:, j * P:(j + 1) * P]
                    pe.matmul(dst, onehotT[:, j * P:(j + 1) * P], b2_sb, start=True, stop=False)
                    for c in range(EC):
                        mm = pe.matmul(dst, hid[:, c, j * P:(j + 1) * P], w2_sb[:, c, :], start=False, stop=(c == EC - 1))
                mm.then_inc(moe_made, 1)
                pe.wait_ge(moe_relu, u + 1)

        def tail_scalar(act, copy_chunks):
            act.wait_ge(score_shown, 1)
            act.activation(score_b, wide[:, 0:N], ACT.Copy).then_inc(score_in, 1)
            with act.Fori(0, T // 4) as u:
                for j in range(4):
                    i = 4 * u + j
                    act.wait_ge(mix_logit, at(mix_logit, i + 1))
                    act.activation(logit[:, j % 2, 0:N], logit[:, j % 2, 0:N], ACT.Exp, bias=mix_nm[:, j:j + 1],
                                   accum_out=mix_sum[:, j:j + 1]).then_inc(mix_exp, 1)
                    copy_chunks([4] * (N // 512), mix_turned, mix_copied, i * (N // 512))
                act.wait_ge(xn3T_made, u + 1)
                act.activation(xn3T, turn[0][:, :].rearrange("p (j n) -> p j n", j=4), ACT.Copy).then_inc(xn3T_in, 1)
                act.wait_ge(hot_turned, u + 1)
                act.activation(onehotT, turn[0][0:E, :], ACT.Copy)
                act.activation(onehotTb, turn[0][0:E, :], ACT.Copy).then_inc(hot_in, 1)
                for c in range(EC):
                    act.wait_ge(hid_made, EC * u + c + 1)
                    act.activation(hid[:, c, :], wide[:, (c % 2) * 512:(c % 2 + 1) * 512], ACT.Relu,
                                   bias=b1_sb[:, c:c + 1]).then_inc(hid_relu, 1)
                act.wait_ge(moe_made, u + 1)
                act.wait_ge(y_free, at(y_free, u))
                act.activation(y_moe, turn[1][:, :].rearrange("p (j n) -> p j n", j=4), ACT.Relu).then_inc(moe_relu, 1)

        def tail_vector(dve, inverse_root):
            dve.drain()
            for t in range(T):
                dve.bn_stats(stats[:, t, :], xn1T[:, t, :])
            dve.drain()
            for t in range(T):
                dve.bn_aggr(moments[:, t, :], stats[:, t, :])
            dve.drain()
            y = inverse_root(moments[:, :, 1], T)
            for t in range(T):
                dve.tensor_scalar(xn1T[:, t, :], xn1T[:, t, :], moments[:, t, 0:1], y[:, t:t + 1], ALU.subtract, ALU.mult)
            dve.drain()
            weighted = att_p[:, 0:N].rearrange("p (t n) -> p t n", n=P)
            dve.tensor_tensor(weighted, xn1T[:, :, :],
                              hv_b[:, :].rearrange("p (o n) -> p o n", o=1).to_broadcast([P, T, P]), ALU.mult)
            dve.drain()
            dve.reduce_sum(scores[:, :], weighted, AX)
            dve.drain()
            dve.tensor_copy(att_p[:, 0:N].rearrange("p (t n) -> p t n", n=P),
                            scores[:, :].rearrange("p (t o) -> p t o", o=1).to_broadcast([P, T, P]))\
               .then_inc(score_rows, 1)
            dve.wait_ge(score_in, 1)
            dve.wait_ge(t_w, 16 * 5)

            def mix_logits(u, j):
                b = j % 2
                dve.wait_ge(t_adj[b], 16 * (2 * u + j // 2 + 1))
                dve.tensor_tensor(logit[:, b, 0:N], adj_sb[:, b, 0:N], score_b, ALU.mult)
                dve.drain()
                dve.tensor_scalar(adj_sb[:, b, 0:N], adj_sb[:, b, 0:N], 0.0, HIDE, ALU.is_equal, ALU.mult)
                dve.drain()
                dve.tensor_tensor_reduce(logit[:, b, 0:N], logit[:, b, 0:N], adj_sb[:, b, 0:N], 1.0, -3e38, ALU.add,
                                         ALU.max, mix_m[:, j:j + 1])
                dve.drain()
                dve.tensor_scalar(mix_any[:, j:j + 1], mix_m[:, j:j + 1], HIDE / 2, None, ALU.is_gt)
                dve.tensor_scalar(mix_nm[:, j:j + 1], mix_m[:, j:j + 1], -1.0, None, ALU.mult).then_inc(mix_logit, 1)

            def mix_out(u, j):
                i = 4 * u + j
                dve.wait_ge(mix_exp, i + 1)
                dve.reciprocal(mix_r[:, j:j + 1], mix_sum[:, j:j + 1])
                dve.drain()
                dve.tensor_tensor(mix_r[:, j:j + 1], mix_r[:, j:j + 1], mix_any[:, j:j + 1], ALU.mult)
                dve.drain()
                dve.wait_ge(mix_summed, i + 1)
                dve.scalar_tensor_tensor(x3[:, j, :], (acc, rowsum)[j % 2][:, 0:P], mix_r[:, j:j + 1], x2_in[:, j, :],
                                         ALU.mult, ALU.add).then_inc(x3_made, 1)

            def group(u, more):
                mix_logits(u, 1)
                dve.wait_ge(t_x2, 16 * (u + 1))
                for j in range(4):
                    mix_out(u, j)
                    if j < 2:
                        mix_logits(u, j + 2)
                dve.drain()
                for j in range(4):
                    dve.bn_stats(stats[:, j, :], x3[:, j, :])
                dve.drain()
                for j in range(4):
                    dve.bn_aggr(moments[:, j, :], stats[:, j, :])
                dve.drain()
                y = inverse_root(moments[:, 0:4, 1], 4)
                for j in range(4):
                    last = dve.tensor_scalar(xn3[:, j, :], x3[:, j, :], moments[:, j, 0:1], y[:, j:j + 1],
                                             ALU.subtract, ALU.mult)
                last.then_inc(xn3_made, 1)
                dve.wait_ge(route_made, u + 1)
                dve.tensor_tensor(rlog, turn[1][:, 0:4 * E].rearrange("p (j e) -> p j e", j=4),
                                  rb_sb.rearrange("p (o e) -> p o e", o=1).to_broadcast([P, 4, E]), ALU.add)
                dve.drain()
                for j in range(4):
                    dve.max(rtop[:, j, :], rlog[:, j, :])
                dve.drain()
                for j in range(4):
                    dve.max_index(rpos[:, j, :], rtop[:, j, :], rlog[:, j, :])
                dve.drain()
                dve.tensor_copy(rposf, rpos)
                dve.drain()
                dve.tensor_tensor(onehot, iota32[:, :].rearrange("p (o e) -> p o e", o=1).to_broadcast([P, 4, E]),
                                  rposf[:, :, 0:1].to_broadcast([P, 4, E]), ALU.is_equal).then_inc(route_hot, 1)
                if more:
                    mix_logits(u + 1, 0)
                for c in range(EC):
                    dve.wait_ge(hid_relu, EC * u + c + 1)
                    dve.tensor_tensor(hid[:, c, :], hid[:, c, :], wide[:, 1024 + (c % 2) * 512:1536 + (c % 2) * 512],
                                      ALU.mult).then_inc(hid_masked, 1)
                dve.wait_ge(moe_relu, u + 1)
                dve.tensor_tensor(y_moe, y_moe, x3, ALU.add).then_inc(moe_out, 1)
                dve.drain()

            mix_logits(0, 0)
            with dve.Fori(0, T // 4 - 1) as u:
                group(u, True)
            group(T // 4 - 1, False)

        block = ctx.enter_context(nc.Block())

        @block.sync
        def _(sp):
            xr = x.rearrange("(t p) d -> p t d", p=P)
            sp.dma_start(x_all, xr).then_inc(c_x, 16)
            sp.dma_start(wt_sb[:, :], WT).then_inc(c_wa_in, 16)
            for q in range(4):
                sp.dma_start(a_col[32 * q:32 * q + 32, :], a).then_inc(c_ab, 16)
            sp.dma_start(gat_w[:, :], W).then_inc(c_w, 16)
            sp.dma_start(wqpkT_sb, WqpkT).then_inc(c_pk, 16)
            sp.dma_start(pkT_sb, pkT).then_inc(c_pk, 16)
            sp.dma_start(masked_dst, adj[0:P, :]).then_inc(c_adj, 16)
            sp.dma_start(gamma_b[:, :], gamma.partition_broadcast(P)).then_inc(c_mem, 16)
            sp.dma_start(beta_b[:, :], beta.partition_broadcast(P)).then_inc(c_mem, 16)
            sp.dma_start(hv_b[:, :], Hv.rearrange("d o -> (d o)").partition_broadcast(P)).then_inc(c_mem, 16)
            sp.dma_start(b1_sb[:, :], b1).then_inc(c_mem, 16)
            sp.dma_start(wq_pair[:, :], Wq[:, 0:2 * P]).then_inc(wq_in, 16)
            sp.dma_start(wo_pair[:, :, :], Wo.rearrange("(h p) d -> p h d", p=P)[:, 0:2, :]).then_inc(wo_in, 16)

            def one_round(st):
                g, t = st["graph"], st["attend"]
                if g is not None:
                    after(sp, x1_made, g)
                    sp.dma_start(xt[:, :], x[ds(g * P, P), :]).then_inc(xt_in, 16)
                if t is not None:
                    if not isinstance(t, int) or t > 0:
                        wait_alone(sp, x2_out, 16 * t)
                    after(sp, xn2_made, t)
                    sp.wait_ge(x1_out, at(x1_out, 16 * (t + 1)))
                    sp.dma_start(y_acc[:, :], x1_dram[ds(t * P, P), :]).then_inc(x1_back, 16)
                    with sp.Fori(0, STEPS) as s:
                        n = STEPS * t + s
                        after_s = (s + 1) % STEPS
                        sp.wait_ge(q_made, at(q_made, n + 1))
                        sp.dma_start(wq_pair[:, :], Wq[:, ds(after_s * 2 * P, 2 * P)]).then_inc(wq_in, 16)
                        sp.wait_ge(y_made, at(y_made, n + 1))
                        sp.dma_start(wo_pair[:, :, :], Wo.rearrange("(h p) d -> p h d", p=P)[:, ds(2 * after_s, 2), :])\
                          .then_inc(wo_in, 16)
                if g is not None:
                    sp.wait_ge(gat_summed, at(gat_summed, STEPS * (g + 1)))
                    sp.dma_start(masked_dst, adj[ds((g + 1) % T * P, P), :]).then_inc(adj_in, 16)
                    sp.wait_ge(x1_made, at(x1_made, g + 1))
                    sp.dma_start(x1_dram[ds(g * P, P), :], x1[:, :]).then_inc(x1_out, 16)
                if t is not None:
                    sp.wait_ge(x2_made, t + 1)
                    sp.dma_start(x2_dram[ds(t * P, P), :], y_acc[:, :]).then_inc(x2_out, 16)

            every_round(sp, one_round)
            tail_sync(sp)

        @block.gpsimd
        def _(pool):
            pool.memset(ident[:, :], 0.0)
            pool.memset(row_head[:, :], 1.0)
            pool.memset(col_head[:, :], 1.0)
            pool.memset(mask_wide[:, :], 0.0)
            pool.memset(sel_head[:, :, :], 0.0)
            pool.iota(iota_i[:, :], [[KEYS_PER_HEAD, H], [0, K]], base=0, channel_multiplier=0).then_inc(c_pool, 1)
            pool.wait_ge(c_pool, 1)
            pool.affine_select(out=ident[:, :], in_=ident[:, :], compare_op=ALU.not_equal, fill=1.0, base=0,
                               pattern=[[-1, P]], channel_multiplier=1)
            pool.affine_select(out=row_head[:, :], in_=row_head[:, :], compare_op=ALU.is_ge, fill=0.0, base=0,
                               pattern=[[-K, H]], channel_multiplier=1)
            pool.affine_select(out=col_head[:, :], in_=col_head[:, :], compare_op=ALU.is_ge, fill=0.0, base=0,
                               pattern=[[-GD, GH]], channel_multiplier=1)
            pool.affine_select(out=mask_wide[:, :], in_=mask_wide[:, :], compare_op=ALU.is_ge, fill=HIDE, base=384,
                               pattern=[[-1, 896]], channel_multiplier=1)
            pool.affine_select(out=sel_head[:, :, :], in_=sel_head[:, :, :], compare_op=ALU.not_equal, fill=1.0,
                               base=0, pattern=[[-1, GH], [0, P]], channel_multiplier=1)
            pool.tensor_copy(head_base[:, :], iota_i[:, :]).then_inc(c_pool, 1)
            pool.wait_ge(c_pool, 2)
            pool.affine_select(out=row_head[:, :], in_=row_head[:, :], compare_op=ALU.is_ge, fill=0.0, base=K - 1,
                               pattern=[[K, H]], channel_multiplier=-1)
            pool.affine_select(out=col_head[:, :], in_=col_head[:, :], compare_op=ALU.is_ge, fill=0.0, base=GD - 1,
                               pattern=[[GD, GH]], channel_multiplier=-1)
            pool.affine_select(out=sel_head[:, :, :], in_=sel_head[:, :, :], compare_op=ALU.not_equal, fill=1.0,
                               base=-32, pattern=[[-1, GH], [0, P]], channel_multiplier=1)
            pool.iota(iota_i[:, :], [[1, P]], base=0, channel_multiplier=0)
            pool.tensor_copy(identb[:, :], ident[:, :]).then_inc(c_pool, 1)
            pool.wait_ge(c_pool, 3)
            pool.affine_select(out=sel_head[:, :, :], in_=sel_head[:, :, :], compare_op=ALU.not_equal, fill=1.0,
                               base=-64, pattern=[[-1, GH], [0, P]], channel_multiplier=1)
            pool.tensor_copy(iota16[:, :], iota_i[:, 0:K])
            pool.tensor_copy(iota32[:, :], iota_i[:, 0:E]).then_inc(c_ident, 1)
            pool.memset(kv[:, 0:T - 4, :], 0.0).then_inc(c_zero, 1)

            def one_round(st):
                r = st["fetch"]
                if r is None:
                    return
                wait_alone(pool, idx_ready, r + 1)
                with pool.Fori(0, STEPS) as s:
                    n = STEPS * r + s
                    for half in range(2):
                        pool.wait_ge(rows_used, at(rows_used, GROUPS * n + (half - 1) * SLOTS))
                        pool.tensor_copy(idx_now[:, half, :],
                                         idxT[:, ds(r % 2, 1), ds(s * TOK + half * SLOTS * GROUP, SLOTS * GROUP)])\
                            .then_inc(idx_copied, 1)
                        pool.wait_ge(idx_copied, at(idx_copied, 2 * n + half + 1))
                        for slot in range(SLOTS):
                            wait_alone(pool, rows_used, GROUPS * n + (half - 1) * SLOTS + slot + 1)
                            for k in range(GROUP):
                                pool.indirect_dma_start(
                                    ring[:, slot, k, :], None, kv_table,
                                    bass.IndirectOffsetOnAxis(idx_now[:, half, slot * GROUP + k:slot * GROUP + k + 1], 0),
                                ).then_inc(row_in[slot], 16)

            every_round(pool, one_round)
            tail_pool(pool)

        @block.tensor
        def _(pe):
            for sem_, n in starts:
                pe.sem_inc(sem_, n)
            pe.wait_ge(c_pk, 32)
            for c in range(2 * H):
                mm = pe.matmul(wide[:, c * P:(c + 1) * P], wqpkT_sb[:, c * P:(c + 1) * P],
                               pkT_sb[:, c * P:(c + 1) * P], start=True, stop=True)
            mm.then_inc(c_mix, 1)
            pe.wait_ge(c_wa_in, 16)
            pe.wait_ge(c_ablock, 1)
            pe.matmul(acc[:, 0:2 * GH], wt_sb[:, :], a_block[:, :], start=True, stop=True).then_inc(c_wa, 1)
            pe.wait_ge(c_xn, 1)
            pe.wait_ge(c_ident, 1)
            pe.wait_ge(c_mix_sb, 1)
            for t in range(T):
                mm = pe.transpose(wide[:, t * P:(t + 1) * P], x_all[:, t, :], ident[:, :])
            mm.then_inc(c_xT, 1)
            pe.wait_ge(c_xT_sb, 1)
            pe.wait_ge(c_wa_sb, 1)
            for t in range(T):
                mm = pe.matmul(acc[:, t * 8:t * 8 + 8], xnT_all[:, t * P:(t + 1) * P], wa[:, :], start=True, stop=True)
            mm.then_inc(c_sd, 1)
            pe.wait_ge(c_w, 16)
            for t in range(T):
                mm = pe.matmul(wide[:, t * P:(t + 1) * P], xnT_all[:, t * P:(t + 1) * P], gat_w[:, :],
                               start=True, stop=True)
            mm.then_inc(c_h, 1)
            pe.wait_ge(c_sd_sb, 1)
            for t in range(T):
                nat = (dst_nat if t < 8 else dst_nat2)[:, (t % 8) * 96:(t % 8) * 96 + 96]
                mm = pe.transpose(turnb[t // 8][0:96, (t % 8) * P:(t % 8 + 1) * P], nat, identb[:, :])
            mm.then_inc(c_d3, 1)
            pe.wait_ge(c_d3_sb, 1)
            pe.wait_ge(c_h_sb, 1)

            def sum_pair(r, s, pair):
                n = STEPS * r + s
                pe.wait_ge(wblock_ready, 2 * n + pair // 2 + 1)
                pe.wait_ge(rows_out, at(rows_out, PAIRS * n + pair))
                for j in (2 * pair, 2 * pair + 1):
                    pe.wait_ge(row_in[j % SLOTS], 16 * GROUP * (GROUPS // SLOTS * n + j // SLOTS + 1))
                    for k in range(GROUP):
                        token = j * GROUP + k - pair // 2 * (TOK // 2)
                        mm = pe.matmul(rowsum[32 * k:32 * k + H, (j % 2) * ROW:(j % 2 + 1) * ROW],
                                       w_block[:, pair // 2, token, :], ring[:, j % SLOTS, k, :], start=True, stop=True)
                    mm.then_inc(rows_used, 1)

            def turn_pair(r, s, pair):
                pe.wait_ge(rows_copied, PAIRS * (STEPS * r + s) + pair + 1)
                for q in range(4):
                    mm = pe.transpose(rowsum[:, q * P:(q + 1) * P], sums_sb[:, q * P:(q + 1) * P], ident[:, :])
                mm.then_inc(rows_turned, 1)

            def turn_and_sum(probs, widths, turned, copied, count, rhs, dst):
                def turns(q):
                    for b in range(widths[q]):
                        col = (4 * q + b) * P
                        mm = pe.transpose(turn[q % 2][:, b * P:(b + 1) * P], probs[:, col:col + P], ident[:, :])
                    mm.then_inc(turned, 1)

                turns(0)
                for q in range(len(widths)):
                    if q + 1 < len(widths):
                        turns(q + 1)
                    pe.wait_ge(copied, count + q + 1)
                    for b in range(widths[q]):
                        mm = pe.matmul(dst, pt_sb[:, q % 2, b * P:(b + 1) * P], rhs(4 * q + b),
                                       start=(q + b == 0), stop=(q == len(widths) - 1 and b == widths[q] - 1))
                return mm

            def one_round(st):
                g, k, r, t = st["graph"], st["pick"], st["fetch"], st["attend"]

                def step(s):
                    def fetch(part, pair):
                        if r is not None:
                            part(r, s, pair)

                    if g is not None:
                        m = STEPS * g + s
                        for c in range(N // 512):
                            mm = pe.matmul(wide[:, c * 512:(c + 1) * 512], sel_head[:, ds(s, 1), :],
                                           dst3[:, c * 512:(c + 1) * 512], start=True, stop=True)
                        mm.then_inc(dst_shown, 1)
                    if t is not None:
                        n = STEPS * t + s
                        pe.wait_ge(wq_in, 16 * (n + 1))
                        for e in range(2):
                            mm = pe.matmul(turn[0][:, e * P:(e + 1) * P], wq_pair[:, e * P:(e + 1) * P],
                                           xn1T[:, ds(t, 1), :], start=True, stop=True)
                        mm.then_inc(q_made, 1)
                    if k is not None:
                        pe.matmul(turn[1][:, :], xT_pick[:, :], mix_keys[:, ds(s * 512, 512)],
                                  start=True, stop=True).then_inc(sims_made, 1)
                    fetch(sum_pair, 0)
                    fetch(turn_pair, 0)
                    if t is not None:
                        keys = lambda e, q, w: kv[:, 4 * q:4 * q + w, ds((2 * s + e) * P, P)]
                        values = lambda e: (lambda b: kv[:, b, ds((2 * s + e) * P + H * P, P)])
                        chunks = st["chunks"] + 2 * len(st["widths"]) * s

                        def s_rows(e):
                            for q, w in enumerate(st["widths"]):
                                mm = pe.matmul(wide[:, q * 512:q * 512 + w * P], qT[:, e, :], keys(e, q, w),
                                               start=True, stop=True)
                            mm.then_inc(s_made, 1)

                        pe.wait_ge(q_in, n + 1)
                        if g is not None:
                            pe.wait_ge(dst_used, m + 1)
                        s_rows(0)
                    if k is not None:
                        pe.wait_ge(sims_in, STEPS * k + s + 1)
                    fetch(sum_pair, 1)
                    if t is not None:
                        after(pe, y_used, n)
                    if g is not None:
                        pe.wait_ge(gat_exp, m + 1)
                        after(pe, gat_out, m)
                        turn_and_sum(masked_dst, [4] * (N // 512), gat_turned, gat_copied, m * (N // 512),
                                     lambda b: h_all[:, b * P:(b + 1) * P],
                                     acc[:, 2 * P:3 * P]).then_inc(gat_summed, 1)
                    fetch(turn_pair, 1)
                    if t is not None:
                        pe.wait_ge(p_made, 2 * n + 1)
                        s_rows(1)
                    fetch(sum_pair, 2)
                    if t is not None:
                        if g is not None:
                            pe.wait_ge(gat_out, at(gat_out, m + 1))
                        turn_and_sum(att_p, st["widths"], p_turned, p_copied, chunks, values(0), acc[:, 0:P])
                    fetch(turn_pair, 2)
                    if t is not None:
                        pe.wait_ge(p_made, 2 * n + 2)
                        turn_and_sum(att_p, st["widths"], p_turned, p_copied, chunks + len(st["widths"]), values(1),
                                     acc[:, P:2 * P]).then_inc(o_made, 1)
                    fetch(sum_pair, 3)
                    if t is not None:
                        pe.wait_ge(o_in, at(o_in, n + 1))
                        for e in range(2):
                            mm = pe.transpose(turn[0][:, e * P:(e + 1) * P], o_sb[:, e, :], ident[:, :])
                        mm.then_inc(oT_made, 1)
                    fetch(turn_pair, 3)
                    if t is not None:
                        pe.wait_ge(oT_in, n + 1)
                        pe.wait_ge(wo_in, 16 * (n + 1))
                        for e in range(2):
                            mm = pe.matmul(acc[:, 384:512], oT_sb[:, e, :], wo_pair[:, e, :],
                                           start=(e == 0), stop=(e == 1))
                        mm.then_inc(y_made, 1)

                if t is not None:
                    wait_alone(pe, k_kept, t + 1)
                    wait_alone(pe, v_kept, t + 1)
                with pe.Fori(0, STEPS) as s:
                    step(s)
                if k is not None:
                    pe.wait_ge(codes_ready, k + 1)
                    pe.transpose(turn[1][:, 0:P], w_tile[:, :], ident[:, :])
                    pe.transpose(turn[1][:, P:2 * P], code_tile[:, :], ident[:, :]).then_inc(codes_turned, 1)
                if r is not None:
                    pe.wait_ge(rows_out, at(rows_out, STEPS * PAIRS * (r + 1)))
                    for h in range(H):
                        mm = pe.transpose(wide[:, h * P:(h + 1) * P], stage[:, 1, h, :], ident[:, :])
                    mm.then_inc(v_turned, 1)
                if g is not None:
                    pe.wait_ge(xn1_made, g + 1)
                    pe.transpose(turn[0][:, 0:P], xn_tmp[:, :], ident[:, :]).then_inc(xn1T_made, 1)
                if k is not None:
                    pe.wait_ge(idx_ready, k + 1)
                if r is not None:
                    pe.wait_ge(v_kept, r + 1)
                if g is not None:
                    pe.wait_ge(xn1T_in, g + 1)

            every_round(pe, one_round)
            tail_tensor(pe, turn_and_sum)

        @block.scalar
        def _(act):
            act.wait_ge(c_mix, 1)
            act.activation(mix_keys[:, :], wide[:, :], ACT.Copy).then_inc(c_mix_sb, 1)
            act.wait_ge(c_xT, 1)
            act.activation(xnT_all, wide[:, 0:N], ACT.Copy).then_inc(c_xT_sb, 1)
            act.wait_ge(c_h, 1)
            act.activation(h_all, wide[:, 0:N], ACT.Copy).then_inc(c_h_sb, 1)
            act.wait_ge(c_d3, 1)
            for i in range(T // 8):
                last = act.activation(dst3[:, i * 1024:(i + 1) * 1024], turnb[i][0:96, :], ACT.Copy)
            last.then_inc(c_d3_sb, 1)

            def copy_chunks(widths, turned, copied, count, between=None):
                for q, w in enumerate(widths):
                    if q == 2 and between:
                        between()
                    act.wait_ge(turned, at(turned, count + q + 1))
                    act.activation(pt_sb[:, q % 2, 0:w * P], turn[q % 2][:, 0:w * P], ACT.Copy).then_inc(copied, 1)

            def copy_pair(r, s, pair):
                act.wait_ge(rows_used, at(rows_used, GROUPS * (STEPS * r + s) + 2 * pair + 2))
                act.activation(sums_sb[:, :], rowsum[:, :], ACT.Copy).then_inc(rows_copied, 1)

            def keep_pair(r, s, pair):
                act.wait_ge(rows_turned, PAIRS * (STEPS * r + s) + pair + 1)
                after(act, k_kept, r)
                turned = rowsum[:, :].rearrange("p (j v k c) -> p j v k c", j=2, v=2, c=32)
                for part in range(2):
                    kept = act.activation(
                        stage[:, part, :, ds(s * TOK + pair * 2 * GROUP, 2 * GROUP)].rearrange("p h (j k) -> p j k h", j=2),
                        turned[:, :, part, :, 0:H], ACT.Copy)
                kept.then_inc(rows_out, 1)

            def one_round(st):
                g, k, r, t = st["graph"], st["pick"], st["fetch"], st["attend"]

                def step(s):
                    def fetch(part, pair):
                        if r is not None:
                            part(r, s, pair)

                    if t is not None:
                        n = STEPS * t + s
                        act.wait_ge(q_made, at(q_made, n + 1))
                        act.activation(qT[:, :, :], turn[0][:, 0:2 * P].rearrange("p (e n) -> p e n", e=2), ACT.Copy,
                                       scale=float(P) ** -0.5).then_inc(q_in, 1)
                    if k is not None:
                        m = STEPS * k + s
                        act.wait_ge(sims_made, m + 1)
                        after(act, picks_done, m)
                        act.activation(sims[:, :, :], turn[1][:, :].rearrange("p (c n) -> p c n", c=4), ACT.Copy)\
                           .then_inc(sims_in, 1)
                    fetch(copy_pair, 0)
                    if g is not None:
                        m = STEPS * g + s
                        act.wait_ge(dst_used, m + 1)
                        if t is not None:
                            after(act, p_turned, st["chunks"] + 2 * len(st["widths"]) * s)
                        act.activation(att_p[:, 0:N], masked_dst, ACT.Relu, bias=gs[:, 6:7], scale=4.0)\
                           .then_inc(gat_bent, 1)
                    fetch(keep_pair, 0)
                    if g is not None:
                        m = STEPS * g + s
                        act.wait_ge(gat_logit, m + 1)
                        act.activation(masked_dst, masked_dst, ACT.Exp, bias=gs[:, 4:5], scale=SLOPE,
                                       accum_out=gat_sum[:, :]).then_inc(gat_exp, 1)
                    fetch(copy_pair, 1)
                    if t is not None:
                        width = sum(st["widths"]) * P
                        chunks = st["chunks"] + 2 * len(st["widths"]) * s

                        def exps(e):
                            act.wait_ge(s_max, 2 * n + e + 1)
                            after(act, p_turned, chunks + e * len(st["widths"]))
                            act.activation(att_p[:, 0:width], wide[:, 0:width], ACT.Exp, bias=att_nm[:, e:e + 1],
                                           accum_out=att_sum[:, e:e + 1]).then_inc(p_made, 1)

                        if g is None:
                            exps(0)
                    if g is not None:
                        copy_chunks([4] * (N // 512), gat_turned, gat_copied, m * (N // 512),
                                    (lambda: exps(0)) if t is not None else None)
                    fetch(keep_pair, 1)
                    if k is not None:
                        act.wait_ge(top_ready, STEPS * k + s + 1)
                        act.activation(top_e[:, :, :], top_d[:, :, :], ACT.Exp).then_inc(top_exp, 1)
                    fetch(copy_pair, 2)
                    if t is not None:
                        copy_chunks(st["widths"], p_turned, p_copied, chunks)
                        exps(1)
                    fetch(keep_pair, 2)
                    if t is not None:
                        copy_chunks(st["widths"], p_turned, p_copied, chunks + len(st["widths"]))
                    fetch(copy_pair, 3)
                    if t is not None:
                        act.wait_ge(oT_made, n + 1)
                        act.activation(oT_sb[:, :, :], turn[0][:, 0:2 * P].rearrange("p (e n) -> p e n", e=2),
                                       ACT.Copy).then_inc(oT_in, 1)
                    fetch(keep_pair, 3)

                with act.Fori(0, STEPS) as s:
                    step(s)
                if r is not None:
                    if isinstance(r, int) and r == 0:
                        act.wait_ge(c_zero, 1)
                    act.wait_ge(v_turned, r + 1)
                    act.activation(kv[:, ds(r, 1), H * P:2 * H * P], wide[:, 0:H * P].rearrange("p (o n) -> p o n", o=1),
                                   ACT.Copy).then_inc(v_kept, 1)
                if k is not None:
                    act.wait_ge(codes_turned, k + 1)
                    after(act, idx_copied, 2 * STEPS * (k - 1))
                    act.activation(wT[:, ds(k % 2, 1), :], turn[1][:, 0:P].rearrange("p (o n) -> p o n", o=1), ACT.Copy)
                    act.activation(idxT[:, ds(k % 2, 1), :], turn[1][:, P:2 * P].rearrange("p (o n) -> p o n", o=1),
                                   ACT.Copy).then_inc(idx_ready, 1)
                if g is not None:
                    act.wait_ge(xn1T_made, g + 1)
                    act.activation(xT_pick[:, :], turn[0][:, 0:P], ACT.Copy)
                    act.activation(xn1T[:, ds(g, 1), :], turn[0][:, 0:P].rearrange("p (o n) -> p o n", o=1), ACT.Copy)\
                       .then_inc(xn1T_in, 1)

            every_round(act, one_round)
            tail_scalar(act, copy_chunks)

        @block.vector
        def _(dve):
            def inverse_root(var, n):
                v, y, q, z = (rs[:, i, 0:n] for i in range(4))
                dve.tensor_scalar(v, var, EPS, None, ALU.add)
                dve.drain()
                dve.tensor_scalar(rs_i[:, 0, 0:n], v.bitcast(I32), 1, None, ALU.logical_shift_right)
                dve.drain()
                dve.tensor_scalar(y.bitcast(I32), rs_i[:, 0, 0:n], -1.0, float(0x5F3759DF), ALU.mult, ALU.add)
                dve.drain()
                for _ in range(3):
                    dve.tensor_tensor(q, y, y, ALU.mult)
                    dve.drain()
                    dve.scalar_tensor_tensor(z, q, -0.5, v, ALU.mult, ALU.mult)
                    dve.drain()
                    dve.scalar_tensor_tensor(y, z, 1.5, y, ALU.add, ALU.mult)
                    dve.drain()
                return y

            def norm(dst, src):
                dve.bn_stats(stats[:, 0, :], src)
                dve.drain()
                dve.bn_aggr(moments[:, 0, :], stats[:, 0, :])
                dve.drain()
                y = inverse_root(moments[:, 0, 1:2], 1)
                return dve.tensor_scalar(dst, src, moments[:, 0, 0:1], y, ALU.subtract, ALU.mult)

            dve.memset(dst_nat[:, 0:768], 0.0)
            dve.memset(dst_nat2[:, 0:768], 0.0)
            dve.memset(rowsum[:, :], 0.0)
            dve.wait_ge(c_ab, 64)
            dve.wait_ge(c_ident, 1)
            for side in range(2):
                last = dve.tensor_scalar(a_block[:, side * GH:(side + 1) * GH], col_head[:, :], a_col[:, side:side + 1],
                                         None, ALU.mult)
            last.then_inc(c_ablock, 1)
            dve.wait_ge(c_x, 16)
            for t in range(T):
                dve.bn_stats(stats[:, t, :], x_all[:, t, :])
            dve.drain()
            for t in range(T):
                dve.bn_aggr(moments[:, t, :], stats[:, t, :])
            dve.drain()
            y = inverse_root(moments[:, :, 1], T)
            for t in range(T):
                last = dve.tensor_scalar(x_all[:, t, :], x_all[:, t, :], moments[:, t, 0:1], y[:, t:t + 1],
                                         ALU.subtract, ALU.mult)
            last.then_inc(c_xn, 1)
            dve.wait_ge(c_wa, 1)
            dve.tensor_copy(wa[:, :], acc[:, 0:2 * GH]).then_inc(c_wa_sb, 1)
            dve.wait_ge(c_adj, 16)
            dve.tensor_scalar(edge_hide, masked_dst, 0.0, HIDE, ALU.is_le, ALU.mult)
            dve.wait_ge(c_sd, 1)
            dve.tensor_copy(src_dst[:, :, :], acc[:, 0:8 * T].rearrange("p (t c) -> p t c", c=8))
            dve.drain()
            left = dst_parts[:, 0:T * GH].rearrange("p (t h) -> p t h", h=GH)
            dve.tensor_copy(left, src_dst[:, :, GH:2 * GH])
            dve.drain()
            for part in range(3):
                for half in range(T // 8):
                    nat = (dst_nat, dst_nat2)[half][:, 0:768].rearrange("p (t c) -> p t c", c=96)
                    last = dve.tensor_copy(nat[:, :, 32 * part:32 * part + GH], left[:, half * 8:half * 8 + 8, :])
                dve.drain()
                if part < 2:
                    for half in range(T // 8):
                        nat = (dst_nat, dst_nat2)[half][:, 0:768].rearrange("p (t c) -> p t c", c=96)
                        rest = left[:, half * 8:half * 8 + 8, :]
                        dve.tensor_tensor(rest, rest, nat[:, :, 32 * part:32 * part + GH], ALU.subtract)
                    dve.drain()
            dve.sem_inc(c_sd_sb, 1)
            dve.wait_ge(c_mem, 64)
            dve.wait_ge(c_d3, 1)

            def weight_block(n, half):
                tokens = TOK // 2
                w = wT[:, :, :].rearrange("p b n -> p (b n)")[:, ds((n * TOK) % (2 * P) + half * tokens, tokens)]
                dve.tensor_tensor(w_block[:, half, :, :],
                                  w.rearrange("p (t o) -> p t o", o=1).to_broadcast([P, tokens, H]),
                                  row_head[:, :].rearrange("p (o h) -> p o h", o=1).to_broadcast([P, tokens, H]),
                                  ALU.mult).then_inc(wblock_ready, 1)

            def graph_logits(g, s):
                m = STEPS * g + s
                dve.tensor_copy(src_now[:, :], src_dst[:, ds(g, 1), ds(s, 1)].rearrange("p a b -> p (a b)"))
                dve.drain()
                dve.tensor_scalar(gs[:, 6:7], src_now[:, :], 4.0, None, ALU.mult)
                dve.tensor_scalar(gs[:, 3:4], src_now[:, :], SLOPE, None, ALU.mult)
                dve.drain()
                wait_alone(dve, dst_shown, m + 1)
                if not isinstance(m, int) or m > 0:
                    wait_alone(dve, gat_summed, m)
                dve.tensor_tensor_reduce(masked_dst, wide[:, 0:N], edge_hide, 1.0, -3e38, ALU.add, ALU.max,
                                         gs[:, 0:1]).then_inc(dst_used, 1)
                dve.drain()
                dve.tensor_scalar(gs[:, 1:2], gs[:, 0:1], src_now[:, :], None, ALU.add)
                dve.drain()
                dve.scalar_tensor_tensor(gs[:, 2:3], gs[:, 1:2], SLOPE, gs[:, 1:2], ALU.mult, ALU.max)
                dve.drain()
                dve.tensor_tensor(gs[:, 4:5], gs[:, 3:4], gs[:, 2:3], ALU.subtract)

            def graph_leaky(g, s):
                dve.wait_ge(gat_bent, STEPS * g + s + 1)
                dve.tensor_tensor(masked_dst, masked_dst, att_p[:, 0:N], ALU.add).then_inc(gat_logit, 1)

            def graph_head_out(g, s):
                m = STEPS * g + s
                dve.wait_ge(gat_exp, m + 1)
                dve.reciprocal(gs[:, 5:6], gat_sum[:, :])
                dve.drain()
                dve.wait_ge(gat_summed, at(gat_summed, m + 1))
                dve.tensor_scalar(g_out[:, ds(s * GD, GD)], acc[:, ds(2 * P + s * GD, GD)], gs[:, 5:6], None, ALU.mult)\
                   .then_inc(gat_out, 1)

            def row_max(st, s, e):
                width = sum(st["widths"]) * P
                wait_alone(dve, s_made, 2 * (STEPS * st["attend"] + s) + e + 1)
                if st["whole"]:
                    part, mask = wide[:, width - 512:width], mask_wide[:, ds((3 - st["i"]) * P, 512)]
                else:
                    part, mask = wide[:, width - P:width], mask_wide[:, 384:512]
                dve.tensor_tensor(part, part, mask, ALU.add)
                dve.drain()
                dve.reduce_max(att_m[:, e:e + 1], wide[:, 0:width], AX)
                dve.drain()
                dve.tensor_scalar(att_nm[:, e:e + 1], att_m[:, e:e + 1], -1.0, None, ALU.mult).then_inc(s_max, 1)

            def pick_keys(k, s):
                wait_alone(dve, sims_in, STEPS * k + s + 1)
                sides = [(e, p) for e in range(2) for p in range(2)]
                left = lambda e, p: scratch[:, (2 * e + p) * P:(2 * e + p + 1) * P]
                for e, p in sides:
                    dve.max(best[:, e, p, 0:8], sims[:, 2 * e + p, :])
                dve.drain()
                for e, p in sides:
                    dve.match_replace(left(e, p), best[:, e, p, 0:8], sims[:, 2 * e + p, :], -3e38)
                for e, p in sides:
                    dve.max_index(place[:, e, p, 0:8], best[:, e, p, 0:8], sims[:, 2 * e + p, :])
                dve.drain()
                for e, p in sides:
                    dve.max(best[:, e, p, 8:16], left(e, p))
                dve.drain()
                for e, p in sides:
                    dve.max_index(place[:, e, p, 8:16], best[:, e, p, 8:16], left(e, p))
                for e in range(2):
                    dve.tensor_tensor(
                        cand[:, e, :].rearrange("p (i j) -> p i j", j=K),
                        best[:, e, 0, :].rearrange("p (i o) -> p i o", o=1).to_broadcast([P, K, K]),
                        best[:, e, 1, :].rearrange("p (o j) -> p o j", o=1).to_broadcast([P, K, K]), ALU.add)
                dve.drain()
                dve.tensor_copy(placef[:, :, :, :], place[:, :, :, :])

            def pick_pairs(k, s):
                rest = lambda e: sims[:, 2 * e:2 * e + 2, :].rearrange("p a n -> p (a n)")
                for e in range(2):
                    dve.max(top[:, e, 0:8], cand[:, e, :])
                dve.drain()
                for e in range(2):
                    dve.match_replace(rest(e), top[:, e, 0:8], cand[:, e, :], -3e38)
                for e in range(2):
                    dve.max_index(pos[:, e, 0:8], top[:, e, 0:8], cand[:, e, :])
                dve.drain()
                for e in range(2):
                    dve.max(top[:, e, 8:16], rest(e))
                dve.drain()
                for e in range(2):
                    last = dve.max_index(pos[:, e, 8:16], top[:, e, 8:16], rest(e))
                last.then_inc(picks_done, 1)
                dve.tensor_tensor(top_d[:, :, :], top[:, :, :], top[:, :, 0:1].to_broadcast([P, 2, K]),
                                  ALU.subtract).then_inc(top_ready, 1)
                dve.drain()

            def pick_rows(k, s):
                dve.tensor_scalar(pos_hi[:, :, :], pos[:, :, :], 4, None, ALU.logical_shift_right)
                dve.tensor_scalar(pos_lo[:, :, :], pos[:, :, :], K - 1, None, ALU.bitwise_and)
                dve.drain()
                for side, (where, key) in enumerate(((pos_hi, key0), (pos_lo, key1))):
                    hit = scratch[:, :].rearrange("p (n j) -> p n j", j=K)
                    dve.tensor_tensor(
                        hit, where[:, :, :].rearrange("p e (n o) -> p (e n) o", o=1).to_broadcast([P, 2 * K, K]),
                        iota16[:, :].rearrange("p (o j) -> p o j", o=1).to_broadcast([P, 2 * K, K]), ALU.is_equal)
                    dve.drain()
                    hit4 = scratch[:, :].rearrange("p (e n j) -> p e n j", e=2, j=K)
                    dve.tensor_tensor(
                        hit4, hit4,
                        placef[:, :, side, :].rearrange("p e (o j) -> p e o j", o=1).to_broadcast([P, 2, K, K]),
                        ALU.mult)
                    dve.drain()
                    dve.reduce_sum(key[:, :, :].rearrange("p e n -> p (e n)"), hit, AX)
                    dve.drain()
                dve.scalar_tensor_tensor(code_tile[:, ds(s * 2 * K, 2 * K)],
                                         key1[:, :, :].rearrange("p e n -> p (e n)"), float(P),
                                         key0[:, :, :].rearrange("p e n -> p (e n)"), ALU.mult, ALU.add)

            def pick_weights(k, s):
                dve.wait_ge(top_exp, STEPS * k + s + 1)
                dve.reduce_sum(top_s[:, 0, :], top_e[:, :, :], AX)
                dve.drain()
                dve.reciprocal(top_s[:, 1, :], top_s[:, 0, :])
                dve.drain()
                dve.tensor_tensor(w_tile[:, ds(s * 2 * K, 2 * K)].rearrange("p (e n) -> p e n", e=2), top_e[:, :, :],
                                  top_s[:, 1, :].rearrange("p (e o) -> p e o", o=1).to_broadcast([P, 2, K]), ALU.mult)

            def one_round(st):
                g, k, r, t = st["graph"], st["pick"], st["fetch"], st["attend"]
                if isinstance(r, int) and r == 0:
                    dve.wait_ge(idx_ready, 1)
                    weight_block(0, 0)

                def step(s):
                    if g is not None:
                        graph_logits(g, s)
                    if r is not None:
                        n = STEPS * r + s
                        dve.wait_ge(rows_used, at(rows_used, GROUPS * n))
                        weight_block(n, 1)
                    if g is not None:
                        graph_leaky(g, s)
                    if t is not None:
                        row_max(st, s, 0)
                    if k is not None:
                        pick_keys(k, s)
                    if g is not None:
                        graph_head_out(g, s)
                    if k is not None:
                        pick_pairs(k, s)
                    if t is not None:
                        row_max(st, s, 1)
                    if k is not None:
                        pick_rows(k, s)
                    if r is not None:
                        dve.wait_ge(rows_used, at(rows_used, GROUPS * n + GROUPS // 2))
                        dve.wait_ge(idx_ready, min(r + 2, T) if isinstance(r, int) else r + 2)
                        weight_block(n + 1, 0)
                    if t is not None:
                        n = STEPS * t + s
                        dve.wait_ge(p_made, 2 * n + 2)
                        dve.reciprocal(att_r[:, :], att_sum[:, :])
                        dve.drain()
                        dve.wait_ge(o_made, n + 1)
                        for e in range(2):
                            last = dve.tensor_scalar(o_sb[:, e, :], acc[:, e * P:(e + 1) * P], att_r[:, e:e + 1], None,
                                                     ALU.mult)
                        last.then_inc(o_in, 1)
                    if k is not None:
                        pick_weights(k, s)
                    if t is not None:
                        dve.wait_ge(y_made, at(y_made, n + 1))
                        dve.wait_ge(x1_back, 16 * (t + 1))
                        dve.tensor_tensor(y_acc[:, :], y_acc[:, :], acc[:, 384:512], ALU.add).then_inc(y_used, 1)
                        dve.drain()

                with dve.Fori(0, STEPS) as s:
                    step(s)
                if k is not None:
                    dve.drain()
                    dve.tensor_tensor(code_tile[:, :], code_tile[:, :], head_base[:, :], ALU.add).then_inc(codes_ready, 1)
                if g is not None:
                    dve.drain()
                    norm(ln_tmp[:, :], g_out[:, :])
                    dve.drain()
                    dve.tensor_tensor(ln_tmp[:, :], ln_tmp[:, :], gamma_b[:, :], ALU.mult)
                    dve.wait_ge(xt_in, 16 * (g + 1))
                    dve.tensor_tensor(xn_tmp[:, :], xt[:, :], beta_b[:, :], ALU.add)
                    dve.drain()
                    after(dve, x1_out, 16 * g)
                    dve.tensor_tensor(x1[:, :], ln_tmp[:, :], xn_tmp[:, :], ALU.add).then_inc(x1_made, 1)
                    dve.drain()
                    norm(xn_tmp[:, :], x1[:, :]).then_inc(xn1_made, 1)
                if r is not None:
                    if isinstance(r, int) and r == 0:
                        dve.wait_ge(c_zero, 1)
                    dve.wait_ge(v_turned, r + 1)
                    dve.tensor_copy(kv[:, ds(r, 1), 0:H * P], stage[:, 0, :, :].rearrange("p (o h) n -> p o (h n)", o=1))\
                       .then_inc(k_kept, 1)
                if t is not None:
                    dve.sem_inc(x2_made, 1)
                    dve.tensor_copy(xn1T[:, ds(t, 1), :], y_acc[:, :].rearrange("p (o n) -> p o n", o=1))\
                       .then_inc(xn2_made, 1)
                if g is not None:
                    dve.wait_ge(adj_in, 16 * (g + 1))
                    dve.tensor_scalar(edge_hide, masked_dst, 0.0, HIDE, ALU.is_le, ALU.mult)
                    dve.drain()

            every_round(dve, one_round)
            tail_vector(dve, inverse_root)


def kernel(x, adj, L0_gnn_W, L0_gnn_a, L0_gnn_gamma, L0_gnn_beta, L0_ffn_Wq_pk, L0_ffn_pk_keys, L0_ffn_Wq,
           L0_ffn_keys_table, L0_ffn_values_table, L0_ffn_Wo, L1_gnn_H_v, L1_ffn_router_w, L1_ffn_router_b,
           L1_ffn_W1, L1_ffn_b1, L1_ffn_W2, L1_ffn_b2):
    import numpy as np
    import concourse.bacc as bacc
    from concourse.bass_utils import run_bass_kernel_spmd

    D = L0_ffn_Wq_pk.shape[0]
    sides, keys, heads, dk = L0_ffn_pk_keys.shape
    E, _, hidden = L1_ffn_W1.shape
    lay = lambda v: np.ascontiguousarray(v)
    arrays = {
        "x": lay(x), "adj": lay(adj), "W": lay(L0_gnn_W), "WT": lay(np.transpose(L0_gnn_W)), "a": lay(np.transpose(np.reshape(L0_gnn_a, (2, -1)))),
        "gamma": lay(L0_gnn_gamma), "beta": lay(L0_gnn_beta),
        "WqpkT": lay(np.transpose(np.reshape(L0_ffn_Wq_pk, (D, sides, heads, dk)), (3, 2, 1, 0))).reshape(dk, -1),
        "pkT": lay(np.transpose(L0_ffn_pk_keys, (3, 2, 0, 1))).reshape(dk, -1),
        "Wq": lay(L0_ffn_Wq),
        "kv_table": np.concatenate([L0_ffn_keys_table, L0_ffn_values_table], axis=1),
        "Wo": lay(L0_ffn_Wo), "Hv": lay(L1_gnn_H_v),
        "router_wT": lay(np.transpose(L1_ffn_router_w)), "router_b": lay(L1_ffn_router_b),
        "W1": lay(np.transpose(L1_ffn_W1, (1, 0, 2))).reshape(D, E * hidden),
        "b1": lay(np.transpose(np.reshape(L1_ffn_b1, (-1, P)))),
        "W2": lay(np.reshape(L1_ffn_W2, (E * hidden, D))), "b2": lay(L1_ffn_b2),
    }
    nc = bacc.Bacc("TRN2", target_bir_lowering=False, num_devices=1, dynamic_dma_scratch_size=15 * 1024)
    in_maps, args = {}, []
    for name, v in arrays.items():
        in_maps[f"in_{name}"] = v
        args.append(nc.dram_tensor(f"in_{name}", v.shape, mybir.dt.from_np(v.dtype), kind="ExternalInput").ap())
    args.append(nc.dram_tensor("out_0", x.shape, F32, kind="ExternalOutput").ap())
    build_network(nc, *args)
    r = run_bass_kernel_spmd(nc, [in_maps], core_ids=[0])
    return r.results[0]["out_0"]
```
